# Optimizing a Trainium2 kernel written in Bass

```python
import numpy as np
import jax
import jax.numpy as jnp

def _softmax(x, axis=-1):
    return jax.nn.softmax(x, axis=axis)

def _gelu(x):
    return jax.nn.gelu(x, approximate=True)

def _silu(x):
    return jax.nn.silu(x)

def _sigmoid(x):
    return jax.nn.sigmoid(x)

def _layernorm(x, axis=-1, eps=1e-05):
    m = jnp.mean(x, axis=axis, keepdims=True)
    v = jnp.var(x, axis=axis, keepdims=True)
    return (x - m) / jnp.sqrt(v + eps)

def _scatter_add(tgt, idx, src, axis=0):
    return tgt.at[idx].add(src)

def _segment_sum(src, seg, n):
    return jax.ops.segment_sum(src, seg, n)
kernel_name = 'mk_seq_preln_d1_jaxref_r8_3b5cac'

def setup_inputs(seed: int=0):
    np.random.seed(seed)
    _w = jnp.asarray

    def _L0_attn_setup():
        import jax, jax.numpy as jnp
        import numpy as np
        B, T, C, H = (2, 256, 128, 16)
        D = C // H

        def _alibi_slopes(n_heads):
            return 2.0 ** (-(8.0 / n_heads) * jnp.arange(1, n_heads + 1, dtype=jnp.float32))
        key = jax.random.key(seed)
        k1, k2, k3 = jax.random.split(key, 3)
        return {'x': jax.random.normal(k1, (B, T, C), dtype=jnp.float32), 'w_attn': jax.random.normal(k2, (C, 3 * C), dtype=jnp.float32) * 0.02, 'b_attn': jnp.zeros((3 * C,), dtype=jnp.float32), 'w_proj': jax.random.normal(k3, (C, C), dtype=jnp.float32) * 0.02, 'b_proj': jnp.zeros((C,), dtype=jnp.float32)}
    _L0_attn_in = _L0_attn_setup()

    def _L0_ffn_setup():
        import jax, jax.numpy as jnp
        import numpy as np
        TEMPERATURE = 0.5
        CAPACITY_FACTOR = 1.25
        TOP_K = 1
        key = jax.random.key(seed)
        ks = jax.random.split(key, 5)
        B, S, D, H, E = (4, 256, 128, 256, 8)
        s = 0.02
        return {'x': jax.random.normal(ks[0], (B, S, D), jnp.float32), 'gate_w': jax.random.normal(ks[1], (E, D), jnp.float32) * s, 'gate_b': jnp.zeros((E,), jnp.float32), 'rms_w': jnp.ones((E,), jnp.float32), 'w1': jax.random.normal(ks[2], (E, D, H), jnp.float32) * s, 'b1': jnp.zeros((E, H), jnp.float32), 'w2': jax.random.normal(ks[3], (E, H, D), jnp.float32) * s, 'b2': jnp.zeros((E, D), jnp.float32)}
    _L0_ffn_in = _L0_ffn_setup()
    _d = {'L0_attn_x': _L0_attn_in['x'], 'L0_attn_w_attn': _L0_attn_in['w_attn'], 'L0_attn_b_attn': _L0_attn_in['b_attn'], 'L0_attn_w_proj': _L0_attn_in['w_proj'], 'L0_attn_b_proj': _L0_attn_in['b_proj'], 'L0_ffn_gate_w': _L0_ffn_in['gate_w'], 'L0_ffn_gate_b': _L0_ffn_in['gate_b'], 'L0_ffn_rms_w': _L0_ffn_in['rms_w'], 'L0_ffn_w1': _L0_ffn_in['w1'], 'L0_ffn_b1': _L0_ffn_in['b1'], 'L0_ffn_w2': _L0_ffn_in['w2'], 'L0_ffn_b2': _L0_ffn_in['b2']}
    _x0 = _d['L0_attn_x']
    _d['L0_attn_x'] = jax.random.normal(jax.random.fold_in(jax.random.key(seed), 1), (4, 512, 128), dtype=_x0.dtype)
    del _x0
    return _d

def reference(L0_attn_x, L0_attn_w_attn, L0_attn_b_attn, L0_attn_w_proj, L0_attn_b_proj, L0_ffn_gate_w, L0_ffn_gate_b, L0_ffn_rms_w, L0_ffn_w1, L0_ffn_b1, L0_ffn_w2, L0_ffn_b2):

    def _L0_attn_ref(x, w_attn, b_attn, w_proj, b_proj):
        import jax, jax.numpy as jnp
        import numpy as np
        B, T, C, H = (2, 256, 128, 16)
        D = C // H

        def _alibi_slopes(n_heads):
            return 2.0 ** (-(8.0 / n_heads) * jnp.arange(1, n_heads + 1, dtype=jnp.float32))
        b, t, c = x.shape
        qkv = (x @ w_attn + b_attn).reshape(b, t, 3, H, D).transpose(2, 0, 3, 1, 4)
        q, k, v = (qkv[0], qkv[1], qkv[2])
        scores = jnp.einsum('bhtd,bhsd->bhts', q, k) / jnp.sqrt(jnp.float32(D))
        slopes = _alibi_slopes(H)
        pos = jnp.arange(t, dtype=scores.dtype)
        scores = scores + slopes[None, :, None, None] * pos[None, None, None, :]
        causal = jnp.tril(jnp.ones((t, t), dtype=bool))
        scores = jnp.where(causal[None, None], scores, -jnp.inf)
        attn = jax.nn.softmax(scores, axis=-1)
        y = jnp.einsum('bhts,bhsd->bhtd', attn, v)
        y = y.transpose(0, 2, 1, 3).reshape(b, t, c)
        return y @ w_proj + b_proj

    def _L0_ffn_ref(x, gate_w, gate_b, rms_w, w1, b1, w2, b2):
        import jax, jax.numpy as jnp
        import numpy as np
        TEMPERATURE = 0.5
        CAPACITY_FACTOR = 1.25
        TOP_K = 1
        B, S, D = x.shape
        E = gate_w.shape[0]
        xf = x.reshape(-1, D)
        N = xf.shape[0]
        logits = xf @ gate_w.T + gate_b
        eps = jnp.finfo(logits.dtype).eps
        ms = jnp.mean(logits * logits, axis=-1, keepdims=True)
        logits = logits * jax.lax.rsqrt(ms + eps) * rms_w
        gates = jax.nn.softmax(logits / TEMPERATURE, axis=-1)
        g, idx = jax.lax.top_k(gates, TOP_K)
        g, idx = (g[:, 0], idx[:, 0])
        capacity = min(int(np.ceil(N * TOP_K / E * CAPACITY_FACTOR)), N)
        counts = jnp.zeros((E,), jnp.int32).at[idx].add(1)
        active = (counts > 0) & (capacity >= 1)
        mask = active[idx].astype(gates.dtype)
        masked = g * mask
        norm_g = masked / (masked + 1e-06)
        h = jax.nn.gelu(jnp.einsum('nd,edh->neh', xf, w1) + b1, approximate=False)
        y = jnp.einsum('neh,ehd->ned', h, w2) + b2
        out = (y * norm_g[:, None, None]).sum(axis=1)
        return out.reshape(B, S, D)
    x = L0_attn_x
    x = x + _L0_attn_ref(_layernorm(x, axis=-1), L0_attn_w_attn, L0_attn_b_attn, L0_attn_w_proj, L0_attn_b_proj)
    x = x + _L0_ffn_ref(_layernorm(x, axis=-1), L0_ffn_gate_w, L0_ffn_gate_b, L0_ffn_rms_w, L0_ffn_w1, L0_ffn_b1, L0_ffn_w2, L0_ffn_b2)
    return x

_drawn_inputs = setup_inputs


def setup_inputs(seed=0):
    import zlib

    import numpy as np

    out = dict(_drawn_inputs(seed))
    spreads = {'L0_attn_b_attn': (0.0, 0.392),
     'L0_attn_b_proj': (0.0, 0.1),
     'L0_ffn_gate_b': (0.0, 0.8),
     'L0_ffn_rms_w': (1.0, 0.6),
     'L0_ffn_b1': (0.0, 0.1),
     'L0_ffn_b2': (0.0, 0.1)}
    factors = {'L0_attn_w_attn': 4.022, 'L0_ffn_gate_w': 8.0}
    for name, (base, spread) in spreads.items():
        noise = np.random.default_rng([zlib.crc32(name.encode()), seed]).standard_normal(out[name].shape)
        drawn = base * np.exp(spread * noise) if base else spread * noise
        out[name] = jnp.asarray(drawn.astype(out[name].dtype))
    for name, factor in factors.items():
        out[name] = (out[name] * factor).astype(out[name].dtype)
    return out
```

```python
from contextlib import ExitStack

import concourse.bass as bass
from concourse import mybir

ALU = mybir.AluOpType
ACT = mybir.ActivationFunctionType
AX = mybir.AxisListType
F32 = mybir.dt.float32
F32R = mybir.dt.float32r
BF16 = mybir.dt.bfloat16
I32 = mybir.dt.int32

P = 128
QUADS = 4
QR = P // QUADS
TERMS = 3
MASKED = -3.0e38
MASKED_SCORE = -1.0e30
EPS_LN = 1e-5
EPS_F32 = 1.1920929e-07
EPS_GATE = 1e-6
RSQRT_GUESS = 0x5F3759DF
KINDS = 3

C_IDENT, C_MASK, C_KEY, C_QUERY = 0, 128, 640, 1152


def block_kernel(nc, x, w_attn, w_proj, w1, w2, columns, rows, consts, out):
    B, T, C = x.shape
    H = 16
    D = C // H
    NT = w2.shape[1]
    E = (columns.shape[1] - NT - 2) // 2
    TB = T // P
    SETS = H // QUADS
    KMAX = TERMS * D + 2
    KEXP = KMAX + 2
    UNITS = KINDS * QUADS
    CHUNKS = [(1, 0, 5), (2, 5, 10), (3, 10, 16)]
    HB = 8
    STACK_LOADS = 16 * 2 * TERMS * QUADS
    assert C == P and T == 512 and D == 8 and NT == 16

    MAX_BLOCKS = [[3], [2, 0], [1]]
    KEY_BLOCKS = [[0], [1, 3], [2]]
    KIND_AT = [0, 512, 1024]
    PCOLS = 1280

    with ExitStack() as ctx:
        def sb(name, shape, dt=F32):
            return ctx.enter_context(nc.sbuf_tensor(name, shape, dt))

        def bank(name):
            return ctx.enter_context(nc.psum_tensor(name, [P, 512], F32))

        def sem(name):
            return ctx.enter_context(nc.semaphore(name))

        cst = sb("cst", [P, C_QUERY + SETS])
        ident = cst[:, C_IDENT:C_IDENT + P]
        zeros = sb("zeros", [P, T])
        ident_bf = sb("ident_bf", [P, P], BF16)
        score_mask = sb("score_mask", [P, P], BF16)
        w_attn_sb = sb("w_attn_sb", [P, 3 * C])
        w_attn_hi = sb("w_attn_hi", [P, 3 * C], F32R)
        w_attn_lo = sb("w_attn_lo", [P, 3 * C], F32R)
        w_proj_sb = sb("w_proj_sb", [P, C])
        w1_sb = sb("w1_sb", [P, NT * P])
        w1_hi = sb("w1_hi", [P, NT * P], F32R)
        w1_lo = sb("w1_lo", [P, NT * P], F32R)
        w2_sb = sb("w2_sb", [P, NT, C])
        cols_sb = sb("cols_sb", [P, 2 * E + NT + 2])
        gate_sb = cols_sb[:, 0:E]
        b2_cols = cols_sb[:, E:2 * E]
        b1_cols = cols_sb[:, 2 * E:2 * E + NT]
        bq = cols_sb[:, 2 * E + NT:2 * E + NT + 1]
        bk = cols_sb[:, 2 * E + NT + 1:2 * E + NT + 2]
        gate_hi = sb("gate_hi", [P, E], F32R)
        gate_lo = sb("gate_lo", [P, E], F32R)
        rows_sb = sb("rows_sb", [P, 2 * C + 2 * E])
        bv_rows = rows_sb[:, 0:C]
        b_proj_rows = rows_sb[:, C:2 * C]
        gate_b_rows = rows_sb[:, 2 * C:2 * C + E]
        rms_rows = rows_sb[:, 2 * C + E:2 * C + 2 * E]
        b2_sum = sb("b2_sum", [P, 1])

        x_in = sb("x_in", [P, TB, C])
        stats1 = sb("stats1", [P, TB, 6])
        mv1 = sb("mv1", [P, TB, 2])
        rstd1 = sb("rstd1", [P, TB])
        xn = sb("xn", [P, TB, C])
        xT_hi = sb("xT_hi", [P, T], F32R)
        xT_lo = sb("xT_lo", [P, T], F32R)
        q_full = sb("q_full", [P, T])
        k_full = sb("k_full", [P, T])
        q_hi = sb("q_hi", [P, T], F32R)
        q_lo = sb("q_lo", [P, T], F32R)
        k_hi = sb("k_hi", [P, T], F32R)
        k_lo = sb("k_lo", [P, T], F32R)
        q_stack = [sb(f"q_stack{i}", [P, SETS, T], F32R) for i in range(2)]
        k_stack = [sb(f"k_stack{i}", [P, SETS, T], F32R) for i in range(2)]
        v_ones = [sb(f"v_ones{i}", [P, TB, SETS, QUADS, QR]) for i in range(2)]

        row_max = sb("row_max", [P, 2, TB * QUADS])
        unused = sb("unused", [P, 2, T])
        m_hi = sb("m_hi", [TB * QUADS, P], F32R)
        m_lo = sb("m_lo", [TB * QUADS, P], F32R)
        probs = sb("probs", [P, 2, QUADS, PCOLS])
        y_raw = sb("y_raw", [P, 2, T])
        rden = sb("rden", [P, 2, TB * QUADS, 2])
        y_norm = sb("y_norm", [P, TB * C])
        yT = sb("yT", [P, T])

        x_res = sb("x_res", [P, TB, C])
        xb_res = sb("xb_res", [P, TB, C])
        x2 = sb("x2", [P, TB, C])
        stats2 = sb("stats2", [P, TB, 6])
        mv2 = sb("mv2", [P, TB, 2])
        rstd2 = sb("rstd2", [P, TB])
        z = sb("z", [P, TB, C])
        zT_hi = sb("zT_hi", [P, T], F32R)
        zT_lo = sb("zT_lo", [P, T], F32R)
        lg = sb("lg", [P, TB, E])
        lg2 = sb("lg2", [P, TB, E])
        lge = sb("lge", [P, TB, E])
        rt = sb("rt", [P, 6, TB])
        hidden = sb("hidden", [P, HB, T])
        ffn_T = sb("ffn_T", [P, T])
        result = sb("result", [P, TB, C])

        v_ring = [bank("v_ring0"), bank("v_ring1")]
        e_ring = [bank("e_ring0"), bank("e_ring1")]
        g_ring = [bank("g_ring0"), bank("g_ring1")]
        pv_bank = bank("pv_bank")
        ffn_bank = bank("ffn_bank")

        x_loaded = sem("x_loaded")
        cst_loaded = sem("cst_loaded")
        wa_loaded = sem("wa_loaded")
        rows_loaded = sem("rows_loaded")
        wp_loaded = sem("wp_loaded")
        w1_loaded = sem("w1_loaded")
        w2_loaded = sem("w2_loaded")
        xres_loaded = sem("xres_loaded")
        stack_loaded = sem("stack_loaded")
        m_loaded = sem("m_loaded")
        stored = sem("stored")
        wa_split = sem("wa_split")
        w1_split = sem("w1_split")
        v_const = sem("v_const")
        zeros_set = sem("zeros_set")
        mask_ready = sem("mask_ready")
        stack_const = sem("stack_const")
        v_filled = sem("v_filled")
        v_freed = sem("v_freed")
        e_filled = sem("e_filled")
        e_freed = sem("e_freed")
        g_filled = sem("g_filled")
        g_freed = sem("g_freed")
        dve_step = sem("dve_step")
        xn_ready = sem("xn_ready")
        xT_ready = sem("xT_ready")
        qk_ready = sem("qk_ready")
        qk_split = sem("qk_split")
        pool_step = sem("pool_step")
        v_ready = sem("v_ready")
        proj_in_read = sem("proj_in_read")
        set_scored = sem("set_scored")
        max_ready = sem("max_ready")
        m_ready = sem("m_ready")
        pv_done = sem("pv_done")
        pv_evacuated = sem("pv_evacuated")
        y_norm_ready = sem("y_norm_ready")
        yT_ready = sem("yT_ready")
        xb_ready = sem("xb_ready")
        z_ready = sem("z_ready")
        zT_ready = sem("zT_ready")
        x2_ready = sem("x2_ready")
        gate_in = sem("gate_in")
        gate_exp = sem("gate_exp")
        ffn1_done = sem("ffn1_done")
        ffn2_done = sem("ffn2_done")
        ffn_evacuated = sem("ffn_evacuated")
        result_ready = sem("result_ready")

        x_view = x.rearrange("b (n p) c -> b p n c", p=P)
        out_view = out.rearrange("b (n p) c -> b p n c", p=P)
        def next_set(b, s):
            return (b, s + 1) if s < SETS - 1 else (b + 1, 0)

        def chunk(b, s):
            for step, lo, hi in CHUNKS:
                if b >= 1 and s == step:
                    return range(lo, hi)
            return range(0)

        block = ctx.enter_context(nc.Block())

        @block.sync
        def _(sp):
            def load_x(b):
                if b >= 1:
                    sp.wait_ge(xn_ready, b)
                sp.dma_start(x_in[:], x_view[b]).then_inc(x_loaded, 16)

            def load_residual(b):
                if b >= 1:
                    sp.wait_ge(xb_ready, b)
                sp.dma_start(x_res[:], x_view[b]).then_inc(xres_loaded, 16)

            def load_stacks(b):
                if b < 2:
                    sp.wait_ge(stack_const, 2 * SETS * (b + 1))
                else:
                    sp.wait_ge(set_scored, SETS * (b - 1))
                for parts, dst, terms in ((q_hi, q_lo), q_stack[b % 2], (0, 0, 1)), ((k_hi, k_lo), k_stack[b % 2], (0, 1, 0)):
                    for part in (0, 1):
                        sp.wait_ge(qk_split, 4 * b + (1 + part if parts[0] is q_hi else 3 + part))
                        for g in range(TERMS):
                            if terms[g] != part:
                                continue
                            for q in range(QUADS):
                                sp.dma_start(dst[QR * q + g * D:QR * q + (g + 1) * D, :, :].bitcast(F32),
                                             parts[part][QR * q:QR * (q + 1), :].bitcast(F32)).then_inc(stack_loaded, 16)

            def load_max(b, s):
                sp.wait_ge(m_ready, SETS * b + s + 1)
                for r, part in ((KMAX, m_hi), (KMAX + 1, m_lo)):
                    sp.dma_start(q_stack[b % 2][r::QR, s, :].bitcast(F32), part[:].bitcast(F32)).then_inc(m_loaded, 16)

            def store(b):
                sp.wait_ge(result_ready, b + 1)
                sp.dma_start(out_view[b], result[:]).then_inc(stored, 16)

            load_x(0)
            sp.dma_start(w_attn_sb[:], w_attn).then_inc(wa_loaded, 16)
            sp.dma_start(cst[:], consts).then_inc(cst_loaded, 16)
            sp.dma_start(cols_sb[:], columns).then_inc(rows_loaded, 16)
            sp.dma_start(rows_sb[:], rows.to_broadcast([P, rows.shape[1]])).then_inc(rows_loaded, 16)
            sp.dma_start(w1_sb[:], w1).then_inc(w1_loaded, 16)
            load_stacks(0)
            sp.dma_start(w_proj_sb[:], w_proj).then_inc(wp_loaded, 16)
            sp.dma_start(w2_sb[:], w2).then_inc(w2_loaded, 16)
            load_residual(0)
            load_x(1)
            for b in range(B):
                for s in range(SETS):
                    load_max(b, s)
                    if s == 0 and b >= 1:
                        load_residual(b)
                        if b >= 2:
                            store(b - 2)
                        if b + 1 < B:
                            load_x(b + 1)
                    if s == 2 and b + 1 < B:
                        load_stacks(b + 1)
            store(B - 2)
            store(B - 1)
            sp.wait_ge(stored, 16 * B)

        @block.gpsimd
        def _(pool):
            def split(src, hi, lo, done, step):
                pool.tensor_copy(hi, src).then_inc(done, 1)
                pool.wait_ge(done, step + 1)
                pool.tensor_tensor(lo, src, hi.bitcast(F32), ALU.subtract).then_inc(done, 1)

            def split_qk(b):
                for n, (full, hi, lo) in enumerate(((q_full, q_hi, q_lo), (k_full, k_hi, k_lo))):
                    pool.wait_ge(qk_ready, 2 * b + n + 1)
                    if b >= 1 and n == 0:
                        pool.wait_ge(stack_loaded, STACK_LOADS * b)
                    split(full[:], hi[:], lo[:], qk_split, 4 * b + 2 * n)

            pool.memset(zeros[:], 0.0).then_inc(zeros_set, 1)
            pool.wait_ge(zeros_set, 1)
            pool.affine_select(out=ident_bf[:], in_=zeros[:, 0:P], compare_op=ALU.not_equal, fill=1.0, base=0,
                               pattern=[[1, P]], channel_multiplier=-1).then_inc(mask_ready, 1)
            pool.affine_select(out=score_mask[:], in_=zeros[:, 0:P], compare_op=ALU.is_ge, fill=MASKED_SCORE, base=0,
                               pattern=[[1, P]], channel_multiplier=-1).then_inc(mask_ready, 1)
            pool.wait_ge(wa_loaded, 16)
            split(w_attn_sb[:], w_attn_hi[:], w_attn_lo[:], wa_split, 0)
            pool.memset(v_ones[0][:], 0.0).then_inc(pool_step, 1)
            pool.wait_ge(pool_step, 1)
            for e in range(2):
                pool.memset(v_ones[0][:].rearrange("p n (s e) q i -> p (n s) e q i", e=2)[:, :, e, :, 16 + 8 * e:24 + 8 * e],
                            1.0).then_inc(v_const, 1)
            split_qk(0)
            pool.memset(v_ones[1][:], 0.0).then_inc(pool_step, 1)
            pool.wait_ge(pool_step, 2)
            for e in range(2):
                pool.memset(v_ones[1][:].rearrange("p n (s e) q i -> p (n s) e q i", e=2)[:, :, e, :, 16 + 8 * e:24 + 8 * e],
                            1.0).then_inc(v_const, 1)

            def residual(b):
                pool.wait_ge(xres_loaded, 16 * (b + 1))
                if b >= 1:
                    pool.wait_ge(x2_ready, b)
                pool.tensor_tensor(xb_res[:], x_res[:], b_proj_rows.unsqueeze(1).to_broadcast([P, TB, C]),
                                   ALU.add).then_inc(xb_ready, 1)

            for b in range(B):
                for s in range(SETS):
                    if s == 1 and b + 1 < B:
                        split_qk(b + 1)
                    if b == 0 and s == 0:
                        pool.wait_ge(w1_loaded, 16)
                        split(w1_sb[:], w1_hi[:], w1_lo[:], w1_split, 0)
                        pool.wait_ge(rows_loaded, 32)
                        split(gate_sb, gate_hi[:], gate_lo[:], w1_split, 2)
                    if s == 2:
                        residual(b)

        @block.scalar
        def _(act):
            def exp_unit(b, s, kind, q):
                n = SETS * b + s
                unit = UNITS * n + QUADS * kind + q
                act.wait_ge(e_filled, unit + 1)
                if n >= 2 and kind == 0 and q == 0:
                    act.wait_ge(pv_done, n - 1)
                cols = 128 * sum(TB - j for j in KEY_BLOCKS[kind])
                act.activation(probs[:, n % 2, q, KIND_AT[kind]:KIND_AT[kind] + cols],
                               e_ring[unit % 2][:, 0:cols], ACT.Exp).then_inc(e_freed, 1)

            def evacuate_pv(b, half):
                act.wait_ge(pv_done, SETS * b + 2 * half + 2)
                if b >= 1:
                    act.wait_ge(y_norm_ready, 2 * (b - 1) + half + 1)
                act.activation(y_raw[:, half, :], pv_bank[:], ACT.Copy).then_inc(pv_evacuated, 1)

            def gelu_tile(b, m):
                n = NT * b + m
                act.wait_ge(g_filled, n + 1)
                if b == 0 and m == 0:
                    act.wait_ge(rows_loaded, 32)
                if n >= HB:
                    act.wait_ge(ffn2_done, n - HB + 1)
                act.activation(hidden[:, n % HB, :], g_ring[n % 2][:], ACT.Gelu,
                               bias=b1_cols[:, m:m + 1]).then_inc(g_freed, 1)

            def evacuate_ffn(b):
                act.wait_ge(ffn2_done, NT * (b + 1))
                if b >= 1:
                    act.wait_ge(result_ready, b)
                act.activation(ffn_T[:], ffn_bank[:], ACT.Identity, bias=b2_sum[:, 0:1]).then_inc(ffn_evacuated, 1)

            def gate_exponentials(b):
                act.wait_ge(gate_in, b + 1)
                act.activation(lge[:], lg2[:], ACT.Exp, scale=2.0).then_inc(gate_exp, 1)

            act.wait_ge(zeros_set, 1)
            act.wait_ge(cst_loaded, 16)
            for i in range(2):
                for s in range(SETS):
                    act.activation(q_stack[i][:, s, :], zeros[:], ACT.Identity,
                                   bias=cst[:, C_QUERY + s:C_QUERY + s + 1]).then_inc(stack_const, 1)
                    act.activation(k_stack[i][:, s, :], cst[:, C_KEY:C_KEY + T], ACT.Copy).then_inc(stack_const, 1)
            for b in range(B):
                for s in range(SETS):
                    if s == 0 and b >= 2:
                        evacuate_ffn(b - 2)
                    for m in chunk(b, s):
                        gelu_tile(b - 1, m)
                    for kind in range(KINDS):
                        for q in range(QUADS):
                            exp_unit(b, s, kind, q)
                    if s == 0 and b >= 1:
                        gate_exponentials(b - 1)
                    if s % 2 == 1:
                        evacuate_pv(b, s // 2)
            evacuate_ffn(B - 2)
            gate_exponentials(B - 1)
            for m in range(NT):
                gelu_tile(B - 1, m)
            evacuate_ffn(B - 1)

        @block.tensor
        def _(pe):
            uses = [0]

            def v_bank():
                n = uses[0]
                uses[0] += 1
                if n >= 2:
                    pe.wait_ge(v_freed, n - 1)
                return v_ring[n % 2]

            def transposes(src, name_in, dst):
                for n in range(TB):
                    last = pe.transpose(dst[:, n * P:(n + 1) * P], src(n), ident)
                return last

            def split_product(dst, lhs, rhs):
                pe.matmul(dst, lhs[0], rhs[0], start=True, stop=False)
                pe.matmul(dst, lhs[0], rhs[1], start=False, stop=False)
                return pe.matmul(dst, lhs[1], rhs[0], start=False, stop=True)

            def transpose_x(b):
                pe.wait_ge(xn_ready, b + 1)
                if b == 0:
                    pe.wait_ge(cst_loaded, 16)
                dst = v_bank()
                for n in range(TB):
                    last = pe.transpose(dst[:, n * P:(n + 1) * P], xn[:, n, :], ident)
                last.then_inc(v_filled, 1)

            def project_qk(b, part):
                if part == 0:
                    pe.wait_ge(xT_ready, b + 1)
                    if b == 0:
                        pe.wait_ge(wa_split, 2)
                cols = slice(part * C, (part + 1) * C)
                dst = v_bank()
                split_product(dst[:], (w_attn_hi[:, cols], w_attn_lo[:, cols]), (xT_hi[:], xT_lo[:])).then_inc(v_filled, 1)

            def project_v(b):
                cols = slice(2 * C, 3 * C)
                dst = v_bank()
                for n in range(TB):
                    tok = slice(n * P, (n + 1) * P)
                    last = split_product(dst[:, tok], (xT_hi[:, tok], xT_lo[:, tok]), (w_attn_hi[:, cols], w_attn_lo[:, cols]))
                last.then_inc(v_filled, 1)

            def max_pair(b, s, k):
                if b == B:
                    return
                if k == 0:
                    pe.wait_ge(stack_loaded, STACK_LOADS * (b + 1))
                for q in (2 * (k // KINDS), 2 * (k // KINDS) + 1):
                    rows = slice(QR * q, QR * q + KMAX)
                    dst = v_bank()
                    at = 0
                    for n in MAX_BLOCKS[k % KINDS]:
                        last = pe.matmul(dst[:, at:at + P * (n + 1)], q_stack[b % 2][rows, s, n * P:(n + 1) * P],
                                         k_stack[b % 2][rows, s, 0:P * (n + 1)], start=True, stop=True,
                                         tile_position=(QR * q, 0))
                        at += P * (n + 1)
                    last.then_inc(v_filled, 1)

            def transpose_max(b, s):
                n = SETS * b + s
                pe.wait_ge(max_ready, n + 1)
                dst = v_bank()
                pe.transpose(dst[0:TB * QUADS, 0:P], row_max[:, n % 2, :], ident).then_inc(v_filled, 1)

            def exp_pair(b, s, k):
                n = SETS * b + s
                kind = k // 2
                if n == 0 and k == 0:
                    pe.wait_ge(mask_ready, 2)
                if k == 0:
                    pe.wait_ge(m_loaded, 32 * (n + 1))
                for q in (2 * (k % 2), 2 * (k % 2) + 1):
                    unit = UNITS * n + QUADS * kind + q
                    if unit >= 2:
                        pe.wait_ge(e_freed, unit - 1)
                    rows = slice(QR * q, QR * q + KEXP)
                    at = 0
                    for j in KEY_BLOCKS[kind]:
                        pe.matmul(e_ring[unit % 2][:, at:at + P * (TB - j)], k_stack[b % 2][rows, s, j * P:(j + 1) * P],
                                  q_stack[b % 2][rows, s, j * P:T], start=(at == 0), stop=False,
                                  tile_position=(QR * q, 0), skip_group_check=True)
                        at += P * (TB - j)
                for q in (2 * (k % 2), 2 * (k % 2) + 1):
                    unit = UNITS * n + QUADS * kind + q
                    blocks = len(KEY_BLOCKS[kind])
                    dst = e_ring[unit % 2][:].rearrange("p (a t) -> p a t", t=P)[:, 0::3, :][:, 0:blocks, :]
                    pe.matmul(dst, ident_bf[:], score_mask[:].unsqueeze(1).to_broadcast([P, blocks, P]),
                              start=False, stop=True, skip_group_check=True).then_inc(e_filled, 1)
                if k == 2 * KINDS - 1:
                    pe.wait_ge(e_filled, UNITS * (n + 1))
                    pe.sem_inc(set_scored, 1)

            def pv(b, s, kind):
                n = SETS * b + s
                pe.wait_ge(e_freed, UNITS * n + QUADS * (kind + 1))
                if kind == 0 and s == 0:
                    pe.wait_ge(v_ready, b + 1)
                    if b == 0:
                        pe.wait_ge(v_const, 2)
                    if b == 1:
                        pe.wait_ge(v_const, 4)
                if kind == 0 and s % 2 == 0 and n >= 2:
                    pe.wait_ge(pv_evacuated, n // 2)
                at = KIND_AT[kind]
                for j in KEY_BLOCKS[kind]:
                    cols = P * (TB - j)
                    for q in range(QUADS):
                        last = pe.matmul(pv_bank[QR * q:QR * (q + 1), j * P:T], v_ones[b % 2][:, j, s, q, :],
                                         probs[:, n % 2, q, at:at + cols],
                                         start=(s % 2 == 0 and j == 0), stop=(s % 2 == 1 and j == 2),
                                         tile_position=(0, QR * q), skip_group_check=True)
                    at += cols
                if kind == KINDS - 1:
                    last.then_inc(pv_done, 1)

            def transpose_y(b, half):
                pe.wait_ge(pv_evacuated, 2 * b + half + 1)
                dst = v_bank()
                for n in range(TB):
                    last = pe.transpose(dst[:, n * P:(n + 1) * P], y_raw[:, half, n * P:(n + 1) * P], ident)
                last.then_inc(v_filled, 1)

            def transpose_y_norm(b):
                pe.wait_ge(y_norm_ready, 2 * (b + 1))
                dst = v_bank()
                for n in range(TB):
                    last = pe.transpose(dst[:, n * P:(n + 1) * P], y_norm[:, n * P:(n + 1) * P], ident)
                last.then_inc(v_filled, 1)

            def project_y(b):
                pe.wait_ge(yT_ready, b + 1)
                if b == 0:
                    pe.wait_ge(wp_loaded, 16)
                dst = v_bank()
                for n in range(TB):
                    last = pe.matmul(dst[:, n * P:(n + 1) * P], yT[:, n * P:(n + 1) * P], w_proj_sb[:],
                                     start=True, stop=True)
                last.then_inc(v_filled, 1)

            def transpose_z(b):
                pe.wait_ge(z_ready, b + 1)
                dst = v_bank()
                for n in range(TB):
                    last = pe.transpose(dst[:, n * P:(n + 1) * P], z[:, n, :], ident)
                last.then_inc(v_filled, 1)

            def logits(b):
                pe.wait_ge(zT_ready, b + 1)
                if b == 0:
                    pe.wait_ge(w1_split, 4)
                dst = v_bank()
                for n in range(TB):
                    tok = slice(n * P, (n + 1) * P)
                    last = split_product(dst[:, n * E:(n + 1) * E], (zT_hi[:, tok], zT_lo[:, tok]), (gate_hi[:], gate_lo[:]))
                last.then_inc(v_filled, 1)

            def ffn1(b, m):
                n = NT * b + m
                if n >= 2:
                    pe.wait_ge(g_freed, n - 1)
                if m == 0:
                    pe.wait_ge(zT_ready, b + 1)
                cols = slice(m * P, (m + 1) * P)
                split_product(g_ring[n % 2][:], (w1_hi[:, cols], w1_lo[:, cols]), (zT_hi[:], zT_lo[:])).then_inc(g_filled, 1)

            def ffn2(b, m):
                n = NT * b + m
                pe.wait_ge(g_freed, n + 1)
                if b == 0 and m == 0:
                    pe.wait_ge(w2_loaded, 16)
                if b >= 1 and m == 0:
                    pe.wait_ge(ffn_evacuated, b)
                pe.matmul(ffn_bank[:], w2_sb[:, m, :], hidden[:, n % HB, :], start=(m == 0),
                          stop=(m == NT - 1)).then_inc(ffn2_done, 1)

            def transpose_ffn(b):
                pe.wait_ge(ffn_evacuated, b + 1)
                dst = v_bank()
                for n in range(TB):
                    last = pe.transpose(dst[:, n * P:(n + 1) * P], ffn_T[:, n * P:(n + 1) * P], ident)
                last.then_inc(v_filled, 1)

            def side(b, s, k):
                if s == 0 and b >= 1:
                    if k == 0 and b >= 2:
                        transpose_ffn(b - 2)
                    if k == 0:
                        transpose_y(b - 1, 0)
                        transpose_y(b - 1, 1)
                    if k == 1:
                        transpose_y_norm(b - 1)
                    if k == 2:
                        project_y(b - 1)
                    if k == 4:
                        transpose_z(b - 1)
                    if k == 6:
                        logits(b - 1)
                if s == 1 and b + 1 < B:
                    if k == 2:
                        transpose_x(b + 1)
                    if k == 4:
                        project_qk(b + 1, 0)
                    if k == 5:
                        project_qk(b + 1, 1)
                    if k == 7:
                        project_v(b + 1)
                tiles = chunk(b, s)
                if k <= 1:
                    for m in tiles[3 * k:3 * k + 3]:
                        ffn1(b - 1, m)
                elif 3 <= k:
                    for m in tiles[k - 3:k - 2]:
                        ffn2(b - 1, m)

            transpose_x(0)
            project_qk(0, 0)
            project_qk(0, 1)
            project_v(0)
            for k in range(2 * KINDS):
                max_pair(0, 0, k)
            for b in range(B):
                for s in range(SETS):
                    transpose_max(b, s)
                    for k in range(9):
                        side(b, s, k)
                        if k < 2 * KINDS:
                            max_pair(*next_set(b, s), k)
                        if 2 <= k < 2 + 2 * KINDS:
                            exp_pair(b, s, k - 2)
                        if k == 5:
                            pv(b, s, 0)
                        if k == 7:
                            pv(b, s, 1)
                    pv(b, s, 2)
            transpose_ffn(B - 2)
            transpose_y(B - 1, 0)
            transpose_y(B - 1, 1)
            transpose_y_norm(B - 1)
            project_y(B - 1)
            transpose_z(B - 1)
            logits(B - 1)
            for m in range(NT + 2):
                if m < NT:
                    ffn1(B - 1, m)
                if m >= 2:
                    ffn2(B - 1, m - 2)
            transpose_ffn(B - 1)

        @block.vector
        def _(dve):
            uses = [0]
            steps = [0]

            def v_bank():
                uses[0] += 1
                dve.wait_ge(v_filled, uses[0])
                return v_ring[(uses[0] - 1) % 2]

            def settle(ins):
                steps[0] += 1
                ins.then_inc(dve_step, 1)
                dve.wait_ge(dve_step, steps[0])

            def split(src, hi, lo, freed, ready):
                settle(dve.tensor_copy(hi, src))
                settle(dve.tensor_tensor(lo, src, hi.bitcast(F32), ALU.subtract))
                dve.sem_inc(freed, 1)
                dve.sem_inc(ready, 1)

            def inverse_sqrt(v, y, t):
                settle(dve.tensor_scalar(t.bitcast(I32), v.bitcast(I32), 1, None, ALU.arith_shift_right))
                settle(dve.tensor_scalar(y.bitcast(I32), t.bitcast(I32), -1, RSQRT_GUESS, ALU.mult, ALU.add))
                for _ in range(3):
                    settle(dve.scalar_tensor_tensor(out=t, in0=y, scalar=-0.5, in1=y, op0=ALU.mult, op1=ALU.mult))
                    settle(dve.tensor_tensor(t, t, v, ALU.mult))
                    settle(dve.scalar_tensor_tensor(out=y, in0=t, scalar=1.5, in1=y, op0=ALU.add, op1=ALU.mult))

            def layernorm(src, stats, mv, rstd, dst, ready):
                for n in range(TB):
                    ins = dve.bn_stats(stats[:, n, :], src[:, n, :])
                settle(ins)
                for n in range(TB):
                    ins = dve.bn_aggr(mv[:, n, :], stats[:, n, :])
                settle(ins)
                settle(dve.tensor_scalar(rt[:, 0, :], mv[:, :, 1], EPS_LN, None, ALU.add))
                inverse_sqrt(rt[:, 0, :], rstd[:], rt[:, 1, :])
                for n in range(TB):
                    ins = dve.tensor_scalar(dst[:, n, :], src[:, n, :], mv[:, n, 0:1], rstd[:, n:n + 1],
                                            ALU.subtract, ALU.mult)
                ins.then_inc(ready, 1)

            def normalise_x(b):
                dve.wait_ge(x_loaded, 16 * (b + 1))
                if b >= 1:
                    dve.wait_ge(xT_ready, b)
                layernorm(x_in, stats1, mv1, rstd1, xn, xn_ready)

            def take_xT(b):
                bank_ = v_bank()
                split(bank_[:], xT_hi[:], xT_lo[:], v_freed, xT_ready)

            def take_q(b):
                bank_ = v_bank()
                if b == 0:
                    dve.wait_ge(rows_loaded, 32)
                else:
                    dve.wait_ge(qk_split, 4 * b)
                settle(dve.tensor_scalar(q_full[:], bank_[:], bq, float(D) ** -0.5, ALU.add, ALU.mult))
                dve.sem_inc(v_freed, 1)
                dve.sem_inc(qk_ready, 1)

            def take_k(b):
                bank_ = v_bank()
                settle(dve.tensor_scalar(k_full[:], bank_[:], bk, None, ALU.add))
                dve.sem_inc(v_freed, 1)
                dve.sem_inc(qk_ready, 1)

            def take_v(b):
                bank_ = v_bank()
                if b < 2:
                    dve.wait_ge(v_const, 2 * (b + 1))
                else:
                    dve.wait_ge(pv_done, SETS * (b - 1))
                for s in range(SETS):
                    at = 8 * (s % 2)
                    src = bank_[:].rearrange("p (n q s i) -> p n q s i", n=TB, q=QUADS, s=SETS)[:, :, :, s, :]
                    bias = bv_rows.rearrange("p (a q s i) -> p a q s i", a=1, q=QUADS, s=SETS)[:, :, :, s, :]
                    ins = dve.tensor_tensor(v_ones[b % 2][:, :, s, :, at:at + D], src,
                                            bias.to_broadcast([P, TB, QUADS, D]), ALU.add)
                settle(ins)
                dve.sem_inc(v_freed, 1)
                dve.sem_inc(v_ready, 1)

            def max_pair(b, s, k):
                if b == B:
                    return
                n = SETS * b + s
                for q in (2 * (k // KINDS), 2 * (k // KINDS) + 1):
                    bank_ = v_bank()
                    at = 0
                    for t in MAX_BLOCKS[k % KINDS]:
                        cols = P * (t + 1)
                        ins = dve.tensor_tensor_reduce(unused[:, (uses[0] - 1) % 2, at:at + cols], bank_[:, at:at + cols],
                                                       cst[:, C_MASK + T - cols:C_MASK + T], 1.0, MASKED,
                                                       ALU.add, ALU.max,
                                                       row_max[:, n % 2, q * TB + t:q * TB + t + 1])
                        at += cols
                    ins.then_inc(v_freed, 1)
                if k == 2 * KINDS - 1:
                    dve.wait_ge(v_freed, uses[0])
                    dve.sem_inc(max_ready, 1)

            def take_max(b, s):
                n = SETS * b + s
                bank_ = v_bank()
                if n >= 1:
                    dve.wait_ge(m_loaded, 32 * n)
                src = bank_[0:TB * QUADS, 0:P]
                settle(dve.tensor_scalar(m_hi[:], src, -1.0, None, ALU.mult))
                settle(dve.scalar_tensor_tensor(out=m_lo[:], in0=src, scalar=-1.0, in1=m_hi[:].bitcast(F32),
                                                op0=ALU.mult, op1=ALU.subtract))
                dve.sem_inc(v_freed, 1)
                dve.sem_inc(m_ready, 1)

            def take_y(b, half):
                bank_ = v_bank()
                rows = bank_[:].rearrange("p (g r) -> p g r", r=QR)
                settle(dve.reciprocal(rden[:, half, :, :], rows[:, :, 16::8]))
                dst = y_norm[:].rearrange("p (g h e i) -> p g h e i", h=2, e=2, i=D)[:, :, half, :, :]
                settle(dve.tensor_tensor(dst, rows[:, :, 0:16].rearrange("p g (e i) -> p g e i", e=2),
                                         rden[:, half, :, :].unsqueeze(3).to_broadcast([P, TB * QUADS, 2, D]), ALU.mult))
                dve.sem_inc(v_freed, 1)
                dve.sem_inc(y_norm_ready, 1)

            def take_yT(b):
                bank_ = v_bank()
                settle(dve.tensor_copy(yT[:], bank_[:]))
                dve.sem_inc(v_freed, 1)
                dve.sem_inc(yT_ready, 1)

            def take_attention(b):
                bank_ = v_bank()
                dve.wait_ge(xb_ready, b + 1)
                settle(dve.tensor_tensor(x2[:], bank_[:].rearrange("p (n c) -> p n c", n=TB), xb_res[:], ALU.add))
                dve.sem_inc(v_freed, 1)
                dve.sem_inc(x2_ready, 1)
                layernorm(x2, stats2, mv2, rstd2, z, z_ready)

            def take_zT(b):
                bank_ = v_bank()
                if b >= 1:
                    dve.wait_ge(g_filled, NT * b)
                split(bank_[:], zT_hi[:], zT_lo[:], v_freed, zT_ready)

            def take_logits(b):
                bank_ = v_bank()
                bc = lambda v: v.unsqueeze(2).to_broadcast([P, TB, E])
                row = lambda v: v.unsqueeze(1).to_broadcast([P, TB, E])
                settle(dve.tensor_tensor(lg[:], bank_[:, 0:TB * E].rearrange("p (n e) -> p n e", n=TB),
                                         row(gate_b_rows), ALU.add))
                dve.sem_inc(v_freed, 1)
                settle(dve.tensor_tensor(lg2[:], lg[:], lg[:], ALU.mult))
                settle(dve.tensor_reduce(rt[:, 0, :], lg2[:], AX.X, ALU.add))
                settle(dve.tensor_scalar(rt[:, 1, :], rt[:, 0, :], 1.0 / E, EPS_F32, ALU.mult, ALU.add))
                inverse_sqrt(rt[:, 1, :], rt[:, 2, :], rt[:, 0, :])
                settle(dve.tensor_tensor(lg2[:], lg[:], bc(rt[:, 2, :]), ALU.mult))
                settle(dve.tensor_tensor(lg[:], lg2[:], row(rms_rows), ALU.mult))
                settle(dve.tensor_reduce(rt[:, 3, :], lg[:], AX.X, ALU.max))
                dve.tensor_tensor(lg2[:], lg[:], bc(rt[:, 3, :]), ALU.subtract).then_inc(gate_in, 1)

            def take_gates(b):
                dve.wait_ge(gate_exp, b + 1)
                settle(dve.tensor_reduce(rt[:, 0, :], lge[:], AX.X, ALU.add))
                settle(dve.reciprocal(rt[:, 1, :], rt[:, 0, :]))
                settle(dve.tensor_scalar(rt[:, 2, :], rt[:, 1, :], EPS_GATE, None, ALU.add))
                settle(dve.reciprocal(rt[:, 3, :], rt[:, 2, :]))
                settle(dve.tensor_tensor(rt[:, 5, :], rt[:, 1, :], rt[:, 3, :], ALU.mult))

            def take_ffn(b):
                bank_ = v_bank()
                if b >= 1:
                    dve.wait_ge(stored, 16 * b)
                for n in range(TB):
                    ins = dve.scalar_tensor_tensor(out=result[:, n, :], in0=bank_[:, n * P:(n + 1) * P],
                                                   scalar=rt[:, 5, n:n + 1], in1=x2[:, n, :],
                                                   op0=ALU.mult, op1=ALU.add)
                settle(ins)
                dve.sem_inc(v_freed, 1)
                dve.sem_inc(result_ready, 1)

            def side(b, s, k):
                if s == 0 and b >= 1:
                    if k == 0 and b >= 2:
                        take_ffn(b - 2)
                    if k == 0:
                        take_y(b - 1, 0)
                        take_y(b - 1, 1)
                    if k == 1:
                        take_yT(b - 1)
                    if k == 2:
                        take_attention(b - 1)
                    if k == 4:
                        take_zT(b - 1)
                    if k == 6:
                        take_logits(b - 1)
                if s == 1 and b >= 1 and k == 0:
                    take_gates(b - 1)
                if s == 1 and b + 1 < B:
                    if k == 0:
                        normalise_x(b + 1)
                    if k == 2:
                        take_xT(b + 1)
                    if k == 4:
                        take_q(b + 1)
                    if k == 5:
                        take_k(b + 1)
                    if k == 7:
                        take_v(b + 1)
                if b == 0 and s == 2 and k == 0:
                    settle(dve.tensor_reduce(b2_sum[:], b2_cols, AX.X, ALU.add))

            normalise_x(0)
            take_xT(0)
            take_q(0)
            take_k(0)
            take_v(0)
            dve.wait_ge(cst_loaded, 16)
            for k in range(2 * KINDS):
                max_pair(0, 0, k)
            for b in range(B):
                for s in range(SETS):
                    take_max(b, s)
                    for k in range(9):
                        side(b, s, k)
                        if k < 2 * KINDS:
                            max_pair(*next_set(b, s), k)
            take_ffn(B - 2)
            take_y(B - 1, 0)
            take_y(B - 1, 1)
            take_yT(B - 1)
            take_attention(B - 1)
            take_zT(B - 1)
            take_logits(B - 1)
            take_gates(B - 1)
            take_ffn(B - 1)


def constants(H, T):
    import numpy as np

    SETS = H // QUADS
    D = P // H
    c = np.zeros((P, C_QUERY + SETS), np.float32)
    c[:, C_IDENT:C_IDENT + P] = np.eye(P)
    c[:, C_MASK + T - P:C_MASK + T] = np.where(np.arange(P)[None, :] > np.arange(P)[:, None], MASKED, 0.0)
    slopes = (2.0 ** (-(8.0 / H) * np.arange(1, H + 1))).astype(np.float32)
    high = (slopes.view(np.uint32) & np.uint32(0xFFFFF000)).view(np.float32)
    for q in range(QUADS):
        row = QR * q + TERMS * D
        c[row:row + 2, C_KEY:C_KEY + T] = np.arange(T)
        c[row + 2:row + 4, C_KEY:C_KEY + T] = 1.0
        for s in range(SETS):
            c[row, C_QUERY + s] = high[QUADS * q + s]
            c[row + 1, C_QUERY + s] = (slopes - high)[QUADS * q + s]
    return c


def qk_order(a):
    import numpy as np

    parts = a.reshape(a.shape[:-1] + (3, QUADS, -1, 8))
    qk = parts[..., 0:2, :, :, :].swapaxes(-1, -2)
    return np.ascontiguousarray(np.concatenate(
        [qk.reshape(a.shape[:-1] + (-1,)), parts[..., 2, :, :, :].reshape(a.shape[:-1] + (-1,))], -1))


def kernel(**inputs):
    import numpy as np
    import concourse.bacc as bacc
    from concourse.bass_utils import run_bass_kernel_spmd

    a = {name: np.ascontiguousarray(v) for name, v in inputs.items()}
    x, w1, w2 = a["L0_attn_x"], a["L0_ffn_w1"], a["L0_ffn_w2"]
    E, C, F = w1.shape
    w_attn, b_attn = qk_order(a["L0_attn_w_attn"]), qk_order(a["L0_attn_b_attn"])
    by_tile = lambda v: v.reshape((E * F // P, P) + v.shape[2:]).swapaxes(0, 1)
    arrays = {
        "x": x,
        "w_attn": w_attn,
        "w_proj": a["L0_attn_w_proj"],
        "w1": w1.swapaxes(0, 1).reshape(C, E * F),
        "w2": by_tile(w2),
        "columns": np.concatenate([a["L0_ffn_gate_w"].T, a["L0_ffn_b2"].T, by_tile(a["L0_ffn_b1"]),
                                   b_attn[:2 * C].reshape(2, C).T], 1),
        "rows": np.concatenate([b_attn[2 * C:], a["L0_attn_b_proj"], a["L0_ffn_gate_b"], a["L0_ffn_rms_w"]])[None],
        "consts": constants(16, x.shape[1]),
    }
    arrays = {name: np.ascontiguousarray(v) for name, v in arrays.items()}

    nc = bacc.Bacc("TRN2", target_bir_lowering=False, num_devices=1)
    args = [nc.dram_tensor(name, v.shape, mybir.dt.from_np(v.dtype), kind="ExternalInput").ap()
            for name, v in arrays.items()]
    args.append(nc.dram_tensor("out", x.shape, F32, kind="ExternalOutput").ap())
    block_kernel(nc, *args)
    r = run_bass_kernel_spmd(nc, [arrays], core_ids=[0])
    return r.results[0]["out"]
```

```python
from contextlib import ExitStack

import concourse.bass as bass
from concourse import mybir

ALU = mybir.AluOpType
ACT = mybir.ActivationFunctionType
AX = mybir.AxisListType
F32 = mybir.dt.float32
F32R = mybir.dt.float32r
BF16 = mybir.dt.bfloat16
I32 = mybir.dt.int32

P = 128
QUADS = 4
QR = P // QUADS
TERMS = 3
MASKED = -3.0e38
MASKED_SCORE = -1.0e30
EPS_LN = 1e-5
EPS_F32 = 1.1920929e-07
EPS_GATE = 1e-6
RSQRT_GUESS = 0x5F3759DF
KINDS = 3

CONST_ROWS = 96
ALIBI_ROWS, MAX_ROWS = 96, 104
C_IDENT, C_MASK, C_KEY, C_QUERY, C_QUAD = 0, 128, 640, 1152, 1156


PLACES = 16
MAX_PLACES = 12
TAKE_MAX_AT = 12
EXP_FROM = 4
PV_AT = (11, 13)
PV_LAST_AT = 1
FFN1_AT = (1, 1, 2, 2, 3)
FFN2_AT = (4, 5, 8, 9, 15)
STAGES = {
    "y_low": (3, 0, 0), "y_high": (0, 3, 1), "y_norm": (0, 5, 1), "attention": (0, 8, 1),
    "z_norm": (0, 14, 1), "z": (0, 15, 1), "logits": (1, 7, 1), "route": (2, 12, 1), "gates": (3, 14, 1),
    "ffn": (1, 0, 2), "x_stats": (1, 0, -1), "x_norm": (1, 6, -1), "x": (1, 8, -1), "k": (1, 12, -1),
    "q": (1, 11, -1), "v": (1, 12, -1), "b2": (2, 2, 0),
}
TILES = (5, 3, 3, 5)
LAST_TILES = (3, 2, 3)
FFN_TAIL_AT, LOGITS_TAIL_AT = 2, 5


def due(b, s, k, batches):
    return [(name, b - behind) for name, (step, place, behind) in STAGES.items()
            if (s, k) == (step, place) and 0 <= b - behind < batches]


def block_kernel(nc, x, w_attn, w_proj, w1, w2, columns, rows, consts, out):
    B, T, C = x.shape
    H = 16
    D = C // H
    NT = w2.shape[1]
    E = (columns.shape[1] - NT - 2) // 2
    TB = T // P
    SETS = H // QUADS
    UNITS = KINDS * QUADS
    HB = 6
    Q_LOADS = 16 * TERMS
    K_LOADS = 16 * 2
    K_LOW_LOADS = 16
    assert C == P and T == 512 and D == 8 and NT == 16

    MAX_BLOCKS = [[3], [2, 0], [1]]
    KEY_BLOCKS = [[0], [1, 3], [2]]
    KIND_AT = [0, 512, 1024]
    PCOLS = 1280

    with ExitStack() as ctx:
        def sb(name, shape, dt=F32):
            return ctx.enter_context(nc.sbuf_tensor(name, shape, dt))

        def bank(name):
            return ctx.enter_context(nc.psum_tensor(name, [P, 512], F32))

        def sem(name):
            return ctx.enter_context(nc.semaphore(name))

        cst = sb("cst", [P, C_QUAD + QUADS])
        ident = cst[:, C_IDENT:C_IDENT + P]
        zeros = sb("zeros", [P, T])
        ident_bf = sb("ident_bf", [P, P], BF16)
        score_mask = sb("score_mask", [P, P], BF16)
        w_attn_sb = sb("w_attn_sb", [P, 3 * C])
        w_attn_hi = sb("w_attn_hi", [P, 3 * C], F32R)
        w_attn_lo = sb("w_attn_lo", [P, 3 * C], F32R)
        w_proj_sb = sb("w_proj_sb", [P, C])
        w1_hi = sb("w1_hi", [P, NT * P], F32R)
        w1_lo = sb("w1_lo", [P, NT * P], F32R)
        w2_sb = sb("w2_sb", [P, NT, C])
        cols_sb = sb("cols_sb", [P, 2 * E + NT + 2])
        gate_sb = cols_sb[:, 0:E]
        b2_cols = cols_sb[:, E:2 * E]
        b1_cols = cols_sb[:, 2 * E:2 * E + NT]
        bq = cols_sb[:, 2 * E + NT:2 * E + NT + 1]
        bk = cols_sb[:, 2 * E + NT + 1:2 * E + NT + 2]
        gate_hi = sb("gate_hi", [P, E], F32R)
        gate_lo = sb("gate_lo", [P, E], F32R)
        rows_sb = sb("rows_sb", [P, 2 * C + 2 * E])
        bv_rows = rows_sb[:, 0:C]
        b_proj_rows = rows_sb[:, C:2 * C]
        gate_b_rows = rows_sb[:, 2 * C:2 * C + E]
        rms_rows = rows_sb[:, 2 * C + E:2 * C + 2 * E]
        b2_sum = sb("b2_sum", [P, 1])

        x_in = sb("x_in", [P, TB, C])
        stats1 = sb("stats1", [P, TB, 6])
        mv1 = sb("mv1", [P, TB, 2])
        rstd1 = sb("rstd1", [P, TB])
        xn = sb("xn", [P, TB, C])
        xT_hi = sb("xT_hi", [P, T], F32R)
        xT_lo = sb("xT_lo", [P, T], F32R)
        q_full = sb("q_full", [P, T])
        k_full = sb("k_full", [P, T])
        q_hi = sb("q_hi", [P, T], F32R)
        q_lo = sb("q_lo", [P, T], F32R)
        k_hi = sb("k_hi", [P, T], F32R)
        k_lo = sb("k_lo", [P, T], F32R)
        q_stack = [sb(f"q_stack{i}", [P, SETS, T], F32R) for i in range(2)]
        k_stack = sb("k_stack", [P, SETS, QUADS, T], F32R)
        v_ones = [sb(f"v_ones{i}", [P, TB, SETS, QUADS, QR]) for i in range(2)]

        row_max = sb("row_max", [P, 2, TB * QUADS])
        unused = sb("unused", [P, 2, T], BF16)
        m_hi = sb("m_hi", [TB * QUADS, P], F32R)
        m_lo = sb("m_lo", [TB * QUADS, P], F32R)
        probs = sb("probs", [P, 2, QUADS, PCOLS])
        y_raw = sb("y_raw", [P, 2, T])
        rden = sb("rden", [P, 2, TB * QUADS, 2])
        y_norm = sb("y_norm", [P, TB * C])
        yT = sb("yT", [P, T])

        x_res = sb("x_res", [P, TB, C])
        xb_res = sb("xb_res", [P, TB, C])
        x2 = [sb(f"x2_{i}", [P, TB, C]) for i in range(2)]
        stats2 = sb("stats2", [P, TB, 6])
        mv2 = sb("mv2", [P, TB, 2])
        rstd2 = sb("rstd2", [P, TB])
        z = sb("z", [P, TB, C])
        zT_hi = sb("zT_hi", [P, T], F32R)
        zT_lo = sb("zT_lo", [P, T], F32R)
        var = sb("var", [P, 2, TB])
        mean_square = sb("mean_square", [P, TB])
        inverse_rms = sb("inverse_rms", [P, TB])
        lg = sb("lg", [P, TB, E])
        lg2 = sb("lg2", [P, TB, E])
        lge = sb("lge", [P, TB, E])
        rt = sb("rt", [P, 4, TB])
        gate = [sb(f"gate{i}", [P, TB]) for i in range(2)]
        hidden = sb("hidden", [P, HB, T])
        w1_sb = hidden[:, 0:NT * P // T, :].rearrange("p n t -> p (n t)")
        ffn_T = sb("ffn_T", [P, T])
        result = sb("result", [P, TB, C])

        v_ring = [bank("v_ring0"), bank("v_ring1")]
        e_ring = [bank("e_ring0"), bank("e_ring1")]
        g_ring = [bank("g_ring0"), bank("g_ring1")]
        pv_bank = bank("pv_bank")
        ffn_bank = bank("ffn_bank")

        x_loaded = sem("x_loaded")
        cst_loaded = sem("cst_loaded")
        wa_loaded = sem("wa_loaded")
        rows_loaded = sem("rows_loaded")
        wp_loaded = sem("wp_loaded")
        w1_loaded = sem("w1_loaded")
        w2_loaded = sem("w2_loaded")
        xres_loaded = sem("xres_loaded")
        q_loaded = sem("q_loaded")
        k_loaded = [[sem(f"k_loaded{half}{q}") for q in range(QUADS)] for half in range(2)]
        k_low_loaded = [[sem(f"k_low_loaded{half}{q}") for q in range(QUADS)] for half in range(2)]
        m_loaded = sem("m_loaded")
        stored = sem("stored")
        wa_split = sem("wa_split")
        w1_split = sem("w1_split")
        v_const = sem("v_const")
        zeros_set = sem("zeros_set")
        mask_ready = sem("mask_ready")
        q_const = sem("q_const")
        k_zeros = sem("k_zeros")
        k_const = sem("k_const")
        v_filled = sem("v_filled")
        v_freed = sem("v_freed")
        e_filled = sem("e_filled")
        e_freed = sem("e_freed")
        g_filled = sem("g_filled")
        g_freed = sem("g_freed")
        dve_step = sem("dve_step")
        xn_ready = sem("xn_ready")
        xT_ready = sem("xT_ready")
        q_ready = sem("q_ready")
        k_ready = sem("k_ready")
        q_split = sem("q_split")
        k_split = sem("k_split")
        pool_step = sem("pool_step")
        v_ready = sem("v_ready")
        proj_in_read = sem("proj_in_read")
        max_ready = sem("max_ready")
        m_ready = sem("m_ready")
        pv_done = sem("pv_done")
        pv_evacuated = sem("pv_evacuated")
        y_norm_ready = sem("y_norm_ready")
        yT_ready = sem("yT_ready")
        xb_ready = sem("xb_ready")
        x_stats_ready = sem("x_stats_ready")
        z_stats_ready = sem("z_stats_ready")
        x_rstd_ready = sem("x_rstd_ready")
        z_rstd_ready = sem("z_rstd_ready")
        square_ready = sem("square_ready")
        logits_normed = sem("logits_normed")
        z_ready = sem("z_ready")
        zT_ready = sem("zT_ready")
        x2_ready = sem("x2_ready")
        gate_in = sem("gate_in")
        gate_exp = sem("gate_exp")
        ffn1_done = sem("ffn1_done")
        ffn2_done = sem("ffn2_done")
        b2_ready = sem("b2_ready")
        ffn_evacuated = sem("ffn_evacuated")
        result_ready = sem("result_ready")

        x_view = x.rearrange("b (n p) c -> b p n c", p=P)
        out_view = out.rearrange("b (n p) c -> b p n c", p=P)
        def q_count(b):
            return Q_LOADS * b + 16 * max(0, b - 2)

        def next_set(b, s):
            return (b, s + 1) if s < SETS - 1 else (b + 1, 0)

        def chunk(b, s):
            n = SETS * b + s - SETS - 1
            if n < 0:
                return 0, range(0)
            sizes = LAST_TILES if b == B - 1 and s > 0 else TILES
            first = sum(sizes[:n % SETS])
            return n // SETS, range(first, first + sizes[n % SETS])

        def send_k(queue, part, half, g, q, loaded):
            rows = QR * q + half * QR // 2
            queue.dma_start(k_stack[QR * g + q * D:QR * g + (q + 1) * D, 2 * half:2 * half + 2, q, :].bitcast(F32),
                            part[rows:rows + QR // 2, :].bitcast(F32)).then_inc(loaded, 16)

        def inverse_sqrt(engine, settle, y, src, scale, eps, v, t):
            settle(engine.tensor_scalar(v, src, scale, eps, ALU.mult, ALU.add))
            settle(engine.tensor_scalar(y.bitcast(I32), v.bitcast(I32), -0.5, float(RSQRT_GUESS), ALU.mult, ALU.add))
            for _ in range(3):
                settle(engine.tensor_tensor(t, y, y, ALU.mult))
                settle(engine.tensor_tensor(t, t, v, ALU.mult))
                settle(engine.tensor_scalar(t, t, -0.5, 1.5, ALU.mult, ALU.add))
                settle(engine.tensor_tensor(y, y, t, ALU.mult))

        block = ctx.enter_context(nc.Block())

        @block.sync
        def _(sp):
            def load_x(b):
                if b >= 1:
                    sp.wait_ge(xn_ready, b)
                sp.dma_start(x_in[:], x_view[b]).then_inc(x_loaded, 16)

            def load_residual(b):
                if b >= 1:
                    sp.wait_ge(xb_ready, b)
                sp.dma_start(x_res[:], x_view[b]).then_inc(xres_loaded, 16)

            def load_q(b):
                if b >= 2:
                    sp.wait_ge(e_filled, UNITS * SETS * (b - 1))
                    sp.dma_start(q_stack[b % 2][MAX_ROWS:MAX_ROWS + 2 * QUADS, :, :].bitcast(F32),
                                 zeros[0:2 * QUADS * SETS, :]).then_inc(q_loaded, 16)
                for g, part in ((0, 0), (1, 0), (2, 1)):
                    sp.wait_ge(q_split, 2 * b + part + 1)
                    sp.dma_start(q_stack[b % 2][QR * g:QR * (g + 1), :, :].bitcast(F32),
                                 (q_hi, q_lo)[part][:].bitcast(F32)).then_inc(q_loaded, 16)

            def load_k(b, half):
                if b == 0:
                    sp.wait_ge(k_zeros, half + 1)
                else:
                    sp.wait_ge(e_filled, UNITS * (SETS * (b - 1) + 2 * half + 2))
                sp.wait_ge(k_split, 2 * b + 1)
                for q in range(QUADS):
                    for g in (0, 2):
                        send_k(sp, k_hi, half, g, q, k_loaded[half][q])

            def load_max(b, s):
                sp.wait_ge(m_ready, SETS * b + s + 1)
                for r, part in ((MAX_ROWS, m_hi), (MAX_ROWS + QUADS, m_lo)):
                    sp.dma_start(q_stack[b % 2][r:r + QUADS, s, :].bitcast(F32), part[:].bitcast(F32)).then_inc(m_loaded, 16)

            def store(b):
                sp.wait_ge(result_ready, b + 1)
                sp.dma_start(out_view[b], result[:]).then_inc(stored, 16)

            load_x(0)
            sp.dma_start(w_attn_sb[:], w_attn).then_inc(wa_loaded, 16)
            sp.dma_start(cst[:], consts).then_inc(cst_loaded, 16)
            sp.dma_start(cols_sb[:], columns).then_inc(rows_loaded, 16)
            sp.dma_start(rows_sb[:], rows.to_broadcast([P, rows.shape[1]])).then_inc(rows_loaded, 16)
            sp.dma_start(w1_sb[:], w1).then_inc(w1_loaded, 16)
            load_q(0)
            load_k(0, 0)
            load_k(0, 1)
            sp.dma_start(w_proj_sb[:], w_proj).then_inc(wp_loaded, 16)
            sp.dma_start(w2_sb[:], w2).then_inc(w2_loaded, 16)
            load_residual(0)
            load_x(1)
            load_max(0, 0)
            for b in range(B):
                for s in range(SETS):
                    if s == 0 and b >= 1:
                        load_k(b, 1)
                        load_residual(b)
                        if b + 1 < B:
                            load_x(b + 1)
                    if s == 1 and b >= 2:
                        store(b - 2)
                    if s == 2 and b + 1 < B:
                        load_k(b + 1, 0)
                        load_q(b + 1)
                    if next_set(b, s)[0] < B:
                        load_max(*next_set(b, s))
            store(B - 2)
            store(B - 1)
            sp.wait_ge(stored, 16 * B)

        @block.gpsimd
        def _(pool):
            def split(src, hi, lo, done, step):
                pool.tensor_copy(hi, src).then_inc(done, 1)
                pool.wait_ge(done, step + 1)
                pool.tensor_tensor(lo, src, hi.bitcast(F32), ALU.subtract).then_inc(done, 1)

            def split_low(b, part):
                full, hi, lo, parts, loads, count = (
                    (k_full, k_hi, k_lo, k_split, k_low_loaded[0] + k_low_loaded[1], K_LOW_LOADS * b),
                    (q_full, q_hi, q_lo, q_split, [q_loaded], q_count(b)))[part]
                pool.wait_ge(parts, 2 * b + 1)
                if b >= 1:
                    for loaded in loads:
                        pool.wait_ge(loaded, count)
                pool.tensor_tensor(lo[:], full[:], hi[:].bitcast(F32), ALU.subtract).then_inc(parts, 1)

            def load_k_low(b, half):
                if b == 0:
                    pool.wait_ge(k_zeros, half + 1)
                else:
                    pool.wait_ge(e_filled, UNITS * (SETS * (b - 1) + 2 * half + 2))
                pool.wait_ge(k_split, 2 * b + 2)
                for q in range(QUADS):
                    send_k(pool, k_lo, half, 1, q, k_low_loaded[half][q])

            steps = [0]

            def settle(ins):
                steps[0] += 1
                ins.then_inc(pool_step, 1)
                pool.wait_ge(pool_step, steps[0])

            def x_rstd(b):
                pool.wait_ge(x_stats_ready, b + 1)
                inverse_sqrt(pool, settle, rstd1[:], mv1[:, :, 1], 1.0, EPS_LN, var[:, 0, :], var[:, 1, :])
                pool.sem_inc(x_rstd_ready, 1)

            def z_rstd(b):
                pool.wait_ge(z_stats_ready, b + 1)
                inverse_sqrt(pool, settle, rstd2[:], mv2[:, :, 1], 1.0, EPS_LN, var[:, 0, :], var[:, 1, :])
                pool.sem_inc(z_rstd_ready, 1)

            def norm_logits(b):
                pool.wait_ge(square_ready, b + 1)
                inverse_sqrt(pool, settle, inverse_rms[:], mean_square[:], 1.0 / E, EPS_F32, var[:, 0, :], var[:, 1, :])
                settle(pool.tensor_tensor(lg2[:], lg[:], inverse_rms[:].unsqueeze(2).to_broadcast([P, TB, E]), ALU.mult))
                pool.tensor_tensor(lg[:], lg2[:], rms_rows.unsqueeze(1).to_broadcast([P, TB, E]),
                                   ALU.mult).then_inc(logits_normed, 1)

            pool.memset(zeros[:], 0.0).then_inc(zeros_set, 1)
            pool.wait_ge(zeros_set, 1)
            pool.affine_select(out=ident_bf[:], in_=zeros[:, 0:P], compare_op=ALU.not_equal, fill=1.0, base=0,
                               pattern=[[1, P]], channel_multiplier=-1).then_inc(mask_ready, 1)
            pool.affine_select(out=score_mask[:], in_=zeros[:, 0:P], compare_op=ALU.is_ge, fill=MASKED_SCORE, base=0,
                               pattern=[[1, P]], channel_multiplier=-1).then_inc(mask_ready, 1)
            pool.memset(k_stack[0:CONST_ROWS, 0:2, :, :].bitcast(F32), 0.0).then_inc(k_zeros, 1)
            pool.wait_ge(wa_loaded, 16)
            split(w_attn_sb[:], w_attn_hi[:], w_attn_lo[:], wa_split, 0)
            settle(pool.memset(v_ones[0][:], 0.0))
            for e in range(2):
                pool.memset(v_ones[0][:].rearrange("p n (s e) q i -> p (n s) e q i", e=2)[:, :, e, :, 16 + 8 * e:24 + 8 * e],
                            1.0).then_inc(v_const, 1)
            pool.memset(k_stack[0:CONST_ROWS, 2:4, :, :].bitcast(F32), 0.0).then_inc(k_zeros, 1)
            split_low(0, 1)
            split_low(0, 0)
            load_k_low(0, 0)
            load_k_low(0, 1)
            settle(pool.memset(v_ones[1][:], 0.0))
            for e in range(2):
                pool.memset(v_ones[1][:].rearrange("p n (s e) q i -> p (n s) e q i", e=2)[:, :, e, :, 16 + 8 * e:24 + 8 * e],
                            1.0).then_inc(v_const, 1)

            def residual(b):
                pool.wait_ge(xres_loaded, 16 * (b + 1))
                if b >= 1:
                    pool.wait_ge(x2_ready, b)
                pool.tensor_tensor(xb_res[:], x_res[:], b_proj_rows.unsqueeze(1).to_broadcast([P, TB, C]),
                                   ALU.add).then_inc(xb_ready, 1)

            for b in range(B):
                for s in range(SETS):
                    if s == 0 and b >= 1:
                        load_k_low(b, 1)
                        z_rstd(b - 1)
                    if s == 1 and b + 1 < B:
                        x_rstd(b + 1)
                        split_low(b + 1, 0)
                        split_low(b + 1, 1)
                    if s == 1 and b >= 1:
                        norm_logits(b - 1)
                    if s == 2 and b + 1 < B:
                        load_k_low(b + 1, 0)
                    if b == 0 and s == 0:
                        pool.wait_ge(w1_loaded, 16)
                        split(w1_sb[:], w1_hi[:], w1_lo[:], w1_split, 0)
                        pool.wait_ge(rows_loaded, 32)
                        split(gate_sb, gate_hi[:], gate_lo[:], w1_split, 2)
                    if s == 2:
                        residual(b)
            norm_logits(B - 1)

        @block.scalar
        def _(act):
            def exp_unit(b, s, kind, q):
                n = SETS * b + s
                unit = UNITS * n + QUADS * kind + q
                act.wait_ge(e_filled, unit + 1)
                if n >= 2 and kind == 0 and q == 0:
                    act.wait_ge(pv_done, n - 1)
                cols = 128 * sum(TB - j for j in KEY_BLOCKS[kind])
                act.activation(probs[:, n % 2, q, KIND_AT[kind]:KIND_AT[kind] + cols],
                               e_ring[unit % 2][:, 0:cols], ACT.Exp).then_inc(e_freed, 1)

            def evacuate_pv(b, half):
                act.wait_ge(pv_done, SETS * b + 2 * half + 2)
                if b >= 1:
                    act.wait_ge(y_norm_ready, 2 * (b - 1) + half + 1)
                act.activation(y_raw[:, half, :], pv_bank[:], ACT.Copy).then_inc(pv_evacuated, 1)

            def gelu_tile(b, m):
                n = NT * b + m
                act.wait_ge(g_filled, n + 1)
                if b == 0 and m == 0:
                    act.wait_ge(rows_loaded, 32)
                    act.wait_ge(w1_split, 2)
                if n >= HB:
                    act.wait_ge(ffn2_done, n - HB + 1)
                act.activation(hidden[:, n % HB, :], g_ring[n % 2][:], ACT.Gelu,
                               bias=b1_cols[:, m:m + 1]).then_inc(g_freed, 1)

            def evacuate_ffn(b):
                act.wait_ge(ffn2_done, NT * (b + 1))
                if b == 0:
                    act.wait_ge(b2_ready, 1)
                else:
                    act.wait_ge(result_ready, b)
                act.activation(ffn_T[:], ffn_bank[:], ACT.Identity, bias=b2_sum[:, 0:1]).then_inc(ffn_evacuated, 1)

            def gate_exponentials(b):
                act.wait_ge(gate_in, b + 1)
                act.activation(lge[:], lg2[:], ACT.Exp, scale=2.0).then_inc(gate_exp, 1)

            def split_high(b, part):
                full, hi, ready, parts, loads, count = (
                    (k_full, k_hi, k_ready, k_split, k_loaded[0] + k_loaded[1], K_LOADS * b),
                    (q_full, q_hi, q_ready, q_split, [q_loaded], q_count(b)))[part]
                act.wait_ge(ready, b + 1)
                if b >= 1:
                    for loaded in loads:
                        act.wait_ge(loaded, count)
                act.activation(hi[:], full[:], ACT.Copy).then_inc(parts, 1)

            def q_constants(i):
                for s in range(SETS):
                    act.activation(q_stack[i][CONST_ROWS:P, s, :], zeros[CONST_ROWS:P, :], ACT.Identity,
                                   bias=cst[CONST_ROWS:P, C_QUERY + s:C_QUERY + s + 1]).then_inc(q_const, 1)

            def k_constants(half):
                for q in range(QUADS):
                    act.activation(k_stack[CONST_ROWS:P, 2 * half:2 * half + 2, q, :],
                                   cst[CONST_ROWS:P, C_KEY:C_KEY + T].unsqueeze(1).to_broadcast([QR, 2, T]),
                                   ACT.Copy, scale=cst[CONST_ROWS:P, C_QUAD + q:C_QUAD + q + 1]).then_inc(k_const, 1)

            act.wait_ge(zeros_set, 1)
            act.wait_ge(cst_loaded, 16)
            q_constants(0)
            k_constants(0)
            split_high(0, 1)
            split_high(0, 0)
            k_constants(1)
            q_constants(1)
            for b in range(B):
                for s in range(SETS):
                    if s == 1 and b >= 2:
                        evacuate_ffn(b - 2)
                    fb, tiles = chunk(b, s)
                    for i, m in enumerate(tiles):
                        if s == 0 and i == 2:
                            evacuate_pv(b - 1, 1)
                        gelu_tile(fb, m)
                    if s == 0 and b >= 1 and not tiles:
                        evacuate_pv(b - 1, 1)
                    if s == 2:
                        evacuate_pv(b, 0)
                    for kind in range(KINDS):
                        for q in range(QUADS):
                            exp_unit(b, s, kind, q)
                        if s == 2 and b >= 1 and kind == 2:
                            gate_exponentials(b - 1)
                        if s == 1 and b + 1 < B and kind >= 1:
                            split_high(b + 1, kind - 1)
            evacuate_pv(B - 1, 1)
            for m in range(sum(LAST_TILES), NT):
                gelu_tile(B - 2, m)
            for m in range(NT):
                gelu_tile(B - 1, m)
                if m == 1:
                    evacuate_ffn(B - 2)
                if m == NT - 3:
                    gate_exponentials(B - 1)
            evacuate_ffn(B - 1)

        @block.tensor
        def _(pe):
            uses = [0]

            def v_bank():
                n = uses[0]
                uses[0] += 1
                if n >= 2:
                    pe.wait_ge(v_freed, n - 1)
                return v_ring[n % 2]

            def split_product(dst, lhs, rhs):
                pe.matmul(dst, lhs[0], rhs[0], start=True, stop=False)
                pe.matmul(dst, lhs[0], rhs[1], start=False, stop=False)
                return pe.matmul(dst, lhs[1], rhs[0], start=False, stop=True)

            def transpose_x(b):
                pe.wait_ge(xn_ready, b + 1)
                if b == 0:
                    pe.wait_ge(cst_loaded, 16)
                dst = v_bank()
                for n in range(TB):
                    last = pe.transpose(dst[:, n * P:(n + 1) * P], xn[:, n, :], ident)
                last.then_inc(v_filled, 1)

            def project_qk(b, part):
                pe.wait_ge(xT_ready, b + 1)
                if b == 0:
                    pe.wait_ge(wa_split, 2)
                cols = slice(part * C, (part + 1) * C)
                dst = v_bank()
                split_product(dst[:], (w_attn_hi[:, cols], w_attn_lo[:, cols]), (xT_hi[:], xT_lo[:])).then_inc(v_filled, 1)

            def project_v(b):
                cols = slice(2 * C, 3 * C)
                dst = v_bank()
                for n in range(TB):
                    tok = slice(n * P, (n + 1) * P)
                    last = split_product(dst[:, tok], (xT_hi[:, tok], xT_lo[:, tok]), (w_attn_hi[:, cols], w_attn_lo[:, cols]))
                last.then_inc(v_filled, 1)

            def max_unit(b, s, k):
                if b == B:
                    return
                if k == 0 and b < 2 and s == 0:
                    pe.wait_ge(q_const, SETS * (b + 1))
                if k == 0 and b == 0 and s % 2 == 0:
                    pe.wait_ge(k_const, QUADS * (s // 2 + 1))
                if k == 0:
                    pe.wait_ge(q_loaded, q_count(b + 1))
                q, kind = k // KINDS, k % KINDS
                if kind == 0 and s % 2 == 0:
                    pe.wait_ge(k_loaded[s // 2][q], K_LOADS * (b + 1))
                    pe.wait_ge(k_low_loaded[s // 2][q], K_LOW_LOADS * (b + 1))
                dst = v_bank()
                at = 0
                for n in MAX_BLOCKS[kind]:
                    last = pe.matmul(dst[:, at:at + P * (n + 1)], q_stack[b % 2][:, s, n * P:(n + 1) * P],
                                     k_stack[:, s, q, 0:P * (n + 1)], start=True, stop=True)
                    at += P * (n + 1)
                last.then_inc(v_filled, 1)

            def transpose_max(b, s):
                n = SETS * b + s
                pe.wait_ge(max_ready, n + 1)
                dst = v_bank()
                pe.transpose(dst[0:TB * QUADS, 0:P], row_max[:, n % 2, :], ident).then_inc(v_filled, 1)

            def exp_unit(b, s, k):
                n = SETS * b + s
                kind, q = k // QUADS, k % QUADS
                if n == 0 and k == 0:
                    pe.wait_ge(mask_ready, 2)
                if k == 0:
                    pe.wait_ge(m_loaded, 32 * (n + 1))
                unit = UNITS * n + k
                if unit >= 2:
                    pe.wait_ge(e_freed, unit - 1)
                at = 0
                for j in KEY_BLOCKS[kind]:
                    pe.matmul(e_ring[unit % 2][:, at:at + P * (TB - j)], k_stack[:, s, q, j * P:(j + 1) * P],
                              q_stack[b % 2][:, s, j * P:T], start=(at == 0), stop=False, skip_group_check=True)
                    at += P * (TB - j)
                blocks = len(KEY_BLOCKS[kind])
                dst = e_ring[unit % 2][:].rearrange("p (a t) -> p a t", t=P)[:, 0::3, :][:, 0:blocks, :]
                pe.matmul(dst, ident_bf[:], score_mask[:].unsqueeze(1).to_broadcast([P, blocks, P]),
                          start=False, stop=True, skip_group_check=True).then_inc(e_filled, 1)

            def pv(b, s, kind):
                n = SETS * b + s
                pe.wait_ge(e_freed, UNITS * n + QUADS * (kind + 1))
                if kind == 0 and s == 0:
                    pe.wait_ge(v_ready, b + 1)
                    if b == 0:
                        pe.wait_ge(v_const, 2)
                    if b == 1:
                        pe.wait_ge(v_const, 4)
                if kind == 0 and s % 2 == 0 and n >= 2:
                    pe.wait_ge(pv_evacuated, n // 2)
                at = KIND_AT[kind]
                for j in KEY_BLOCKS[kind]:
                    cols = P * (TB - j)
                    for q in range(QUADS):
                        last = pe.matmul(pv_bank[QR * q:QR * (q + 1), j * P:T], v_ones[b % 2][:, j, s, q, :],
                                         probs[:, n % 2, q, at:at + cols],
                                         start=(s % 2 == 0 and j == 0), stop=(s % 2 == 1 and j == 2),
                                         tile_position=(0, QR * q), skip_group_check=True)
                    at += cols
                if kind == KINDS - 1:
                    last.then_inc(pv_done, 1)

            def transpose_y(b, half):
                pe.wait_ge(pv_evacuated, 2 * b + half + 1)
                dst = v_bank()
                for n in range(TB):
                    last = pe.transpose(dst[:, n * P:(n + 1) * P], y_raw[:, half, n * P:(n + 1) * P], ident)
                last.then_inc(v_filled, 1)

            def transpose_y_norm(b):
                pe.wait_ge(y_norm_ready, 2 * (b + 1))
                dst = v_bank()
                for n in range(TB):
                    last = pe.transpose(dst[:, n * P:(n + 1) * P], y_norm[:, n * P:(n + 1) * P], ident)
                last.then_inc(v_filled, 1)

            def project_y(b):
                pe.wait_ge(yT_ready, b + 1)
                if b == 0:
                    pe.wait_ge(wp_loaded, 16)
                dst = v_bank()
                for n in range(TB):
                    last = pe.matmul(dst[:, n * P:(n + 1) * P], yT[:, n * P:(n + 1) * P], w_proj_sb[:],
                                     start=True, stop=True)
                last.then_inc(v_filled, 1)

            def transpose_z(b):
                pe.wait_ge(z_ready, b + 1)
                dst = v_bank()
                for n in range(TB):
                    last = pe.transpose(dst[:, n * P:(n + 1) * P], z[:, n, :], ident)
                last.then_inc(v_filled, 1)

            def logits(b):
                pe.wait_ge(zT_ready, b + 1)
                if b == 0:
                    pe.wait_ge(w1_split, 4)
                dst = v_bank()
                for n in range(TB):
                    tok = slice(n * P, (n + 1) * P)
                    last = split_product(dst[:, n * E:(n + 1) * E], (zT_hi[:, tok], zT_lo[:, tok]), (gate_hi[:], gate_lo[:]))
                last.then_inc(v_filled, 1)

            def ffn1(b, m):
                n = NT * b + m
                if n >= 2:
                    pe.wait_ge(g_freed, n - 1)
                if m == 0:
                    pe.wait_ge(zT_ready, b + 1)
                cols = slice(m * P, (m + 1) * P)
                split_product(g_ring[n % 2][:], (w1_hi[:, cols], w1_lo[:, cols]), (zT_hi[:], zT_lo[:])).then_inc(g_filled, 1)

            def ffn2(b, m):
                n = NT * b + m
                pe.wait_ge(g_freed, n + 1)
                if b == 0 and m == 0:
                    pe.wait_ge(w2_loaded, 16)
                if b >= 1 and m == 0:
                    pe.wait_ge(ffn_evacuated, b)
                pe.matmul(ffn_bank[:], w2_sb[:, m, :], hidden[:, n % HB, :], start=(m == 0),
                          stop=(m == NT - 1)).then_inc(ffn2_done, 1)

            def transpose_ffn(b):
                pe.wait_ge(ffn_evacuated, b + 1)
                dst = v_bank()
                for n in range(TB):
                    last = pe.transpose(dst[:, n * P:(n + 1) * P], ffn_T[:, n * P:(n + 1) * P], ident)
                last.then_inc(v_filled, 1)

            def side(b, s, k):
                for stage, of in due(b, s, k, B):
                    if stage == "y_low":
                        transpose_y(of, 0)
                    if stage == "y_high":
                        transpose_y(of, 1)
                    if stage == "y_norm":
                        transpose_y_norm(of)
                    if stage == "attention":
                        project_y(of)
                    if stage == "z":
                        transpose_z(of)
                    if stage == "logits":
                        logits(of)
                    if stage == "ffn":
                        transpose_ffn(of)
                    if stage == "x":
                        transpose_x(of)
                    if stage == "q":
                        project_qk(of, 0)
                    if stage == "k":
                        project_qk(of, 1)
                    if stage == "v":
                        project_v(of)
                fb, tiles = chunk(b, s)
                for m, at in zip(tiles, FFN1_AT):
                    if k == at:
                        ffn1(fb, m)
                for m, at in zip(tiles, FFN2_AT):
                    if k == at:
                        ffn2(fb, m)

            transpose_x(0)
            project_qk(0, 0)
            project_qk(0, 1)
            project_v(0)
            for k in range(MAX_PLACES):
                max_unit(0, 0, k)
            transpose_max(0, 0)
            for b in range(B):
                for s in range(SETS):
                    n = SETS * b + s
                    for k in range(PLACES):
                        side(b, s, k)
                        if k < MAX_PLACES:
                            max_unit(*next_set(b, s), k)
                        if k == TAKE_MAX_AT and next_set(b, s)[0] < B:
                            transpose_max(*next_set(b, s))
                        if k >= EXP_FROM:
                            exp_unit(b, s, k - EXP_FROM)
                        if k in PV_AT:
                            pv(b, s, PV_AT.index(k))
                        if k == PV_LAST_AT and n >= 1:
                            pv((n - 1) // SETS, (n - 1) % SETS, KINDS - 1)
            pv(B - 1, SETS - 1, KINDS - 1)
            tiles = range(sum(LAST_TILES), NT)
            for i, m in enumerate(tiles):
                ffn1(B - 2, m)
                if i >= 2:
                    ffn2(B - 2, m - 2)
                if i == 1:
                    transpose_y(B - 1, 1)
                if i == 2:
                    transpose_y_norm(B - 1)
                if i == 3:
                    project_y(B - 1)
            ffn2(B - 2, NT - 2)
            transpose_z(B - 1)
            ffn2(B - 2, NT - 1)
            for m in range(NT + 2):
                if m < NT:
                    ffn1(B - 1, m)
                if m == FFN_TAIL_AT:
                    transpose_ffn(B - 2)
                if m >= 2:
                    ffn2(B - 1, m - 2)
                if m == LOGITS_TAIL_AT:
                    logits(B - 1)
            transpose_ffn(B - 1)

        @block.vector
        def _(dve):
            uses = [0]
            steps = [0]

            def v_bank():
                uses[0] += 1
                dve.wait_ge(v_filled, uses[0])
                return v_ring[(uses[0] - 1) % 2]

            def settle(ins):
                steps[0] += 1
                ins.then_inc(dve_step, 1)
                dve.wait_ge(dve_step, steps[0])

            def split(src, hi, lo, freed, ready):
                settle(dve.tensor_copy(hi, src))
                settle(dve.tensor_tensor(lo, src, hi.bitcast(F32), ALU.subtract))
                dve.sem_inc(freed, 1)
                dve.sem_inc(ready, 1)

            def statistics(src, stats, mv, ready):
                for n in range(TB):
                    ins = dve.bn_stats(stats[:, n, :], src[:, n, :])
                settle(ins)
                for n in range(TB):
                    ins = dve.bn_aggr(mv[:, n, :], stats[:, n, :])
                ins.then_inc(ready, 1)

            def normalise(src, mv, rstd, dst, ready):
                for n in range(TB):
                    ins = dve.tensor_scalar(dst[:, n, :], src[:, n, :], mv[:, n, 0:1], rstd[:, n:n + 1],
                                            ALU.subtract, ALU.mult)
                ins.then_inc(ready, 1)

            def take_x(b):
                dve.wait_ge(x_loaded, 16 * (b + 1))
                if b >= 1:
                    dve.wait_ge(xn_ready, b)
                statistics(x_in, stats1, mv1, x_stats_ready)

            def root_x():
                dve.wait_ge(x_stats_ready, 1)
                inverse_sqrt(dve, settle, rstd1[:], mv1[:, :, 1], 1.0, EPS_LN, rt[:, 0, :], rt[:, 1, :])
                dve.sem_inc(x_rstd_ready, 1)

            def root_z(b):
                dve.wait_ge(z_stats_ready, b + 1)
                inverse_sqrt(dve, settle, rstd2[:], mv2[:, :, 1], 1.0, EPS_LN, rt[:, 0, :], rt[:, 1, :])
                dve.sem_inc(z_rstd_ready, 1)

            def normalise_x(b):
                dve.wait_ge(x_stats_ready, b + 1)
                dve.wait_ge(x_rstd_ready, b + 1)
                if b >= 1:
                    dve.wait_ge(xT_ready, b)
                normalise(x_in, mv1, rstd1, xn, xn_ready)

            def normalise_z(b):
                dve.wait_ge(z_stats_ready, b + 1)
                dve.wait_ge(z_rstd_ready, b + 1)
                normalise(x2[b % 2], mv2, rstd2, z, z_ready)

            def take_xT(b):
                bank_ = v_bank()
                split(bank_[:], xT_hi[:], xT_lo[:], v_freed, xT_ready)

            def take_q(b):
                bank_ = v_bank()
                if b == 0:
                    dve.wait_ge(rows_loaded, 32)
                else:
                    dve.wait_ge(q_split, 2 * b)
                settle(dve.tensor_scalar(q_full[:], bank_[:], bq, float(D) ** -0.5, ALU.add, ALU.mult))
                dve.sem_inc(v_freed, 1)
                dve.sem_inc(q_ready, 1)

            def take_k(b):
                bank_ = v_bank()
                if b >= 1:
                    dve.wait_ge(k_split, 2 * b)
                settle(dve.tensor_scalar(k_full[:], bank_[:], bk, None, ALU.add))
                dve.sem_inc(v_freed, 1)
                dve.sem_inc(k_ready, 1)

            def take_v(b):
                bank_ = v_bank()
                if b < 2:
                    dve.wait_ge(v_const, 2 * (b + 1))
                else:
                    dve.wait_ge(pv_done, SETS * (b - 1))
                for s in range(SETS):
                    at = 8 * (s % 2)
                    src = bank_[:].rearrange("p (n q s i) -> p n q s i", n=TB, q=QUADS, s=SETS)[:, :, :, s, :]
                    bias = bv_rows.rearrange("p (a q s i) -> p a q s i", a=1, q=QUADS, s=SETS)[:, :, :, s, :]
                    ins = dve.tensor_tensor(v_ones[b % 2][:, :, s, :, at:at + D], src,
                                            bias.to_broadcast([P, TB, QUADS, D]), ALU.add)
                settle(ins)
                dve.sem_inc(v_freed, 1)
                dve.sem_inc(v_ready, 1)

            def max_unit(b, s, k):
                if b == B:
                    return
                n = SETS * b + s
                q, kind = k // KINDS, k % KINDS
                bank_ = v_bank()
                at = 0
                for t in MAX_BLOCKS[kind]:
                    cols = P * (t + 1)
                    ins = dve.tensor_tensor_reduce(unused[:, (uses[0] - 1) % 2, at:at + cols], bank_[:, at:at + cols],
                                                   cst[:, C_MASK + T - cols:C_MASK + T], 1.0, MASKED,
                                                   ALU.add, ALU.max,
                                                   row_max[:, n % 2, q * TB + t:q * TB + t + 1])
                    at += cols
                ins.then_inc(v_freed, 1)
                if k == MAX_PLACES - 1:
                    dve.wait_ge(v_freed, uses[0])
                    dve.sem_inc(max_ready, 1)

            def take_max(b, s):
                n = SETS * b + s
                bank_ = v_bank()
                if n >= 1:
                    dve.wait_ge(m_loaded, 32 * n)
                src = bank_[0:TB * QUADS, 0:P]
                settle(dve.tensor_scalar(m_hi[:], src, -1.0, None, ALU.mult))
                settle(dve.scalar_tensor_tensor(out=m_lo[:], in0=src, scalar=-1.0, in1=m_hi[:].bitcast(F32),
                                                op0=ALU.mult, op1=ALU.subtract))
                dve.sem_inc(v_freed, 1)
                dve.sem_inc(m_ready, 1)

            def take_y(b, half):
                bank_ = v_bank()
                rows = bank_[:].rearrange("p (g r) -> p g r", r=QR)
                settle(dve.reciprocal(rden[:, half, :, :], rows[:, :, 16::8]))
                dst = y_norm[:].rearrange("p (g h e i) -> p g h e i", h=2, e=2, i=D)[:, :, half, :, :]
                settle(dve.tensor_tensor(dst, rows[:, :, 0:16].rearrange("p g (e i) -> p g e i", e=2),
                                         rden[:, half, :, :].unsqueeze(3).to_broadcast([P, TB * QUADS, 2, D]), ALU.mult))
                dve.sem_inc(v_freed, 1)
                dve.sem_inc(y_norm_ready, 1)

            def take_yT(b):
                bank_ = v_bank()
                settle(dve.tensor_copy(yT[:], bank_[:]))
                dve.sem_inc(v_freed, 1)
                dve.sem_inc(yT_ready, 1)

            def take_attention(b):
                bank_ = v_bank()
                dve.wait_ge(xb_ready, b + 1)
                settle(dve.tensor_tensor(x2[b % 2][:], bank_[:].rearrange("p (n c) -> p n c", n=TB), xb_res[:], ALU.add))
                dve.sem_inc(v_freed, 1)
                dve.sem_inc(x2_ready, 1)
                statistics(x2[b % 2], stats2, mv2, z_stats_ready)

            def take_zT(b):
                bank_ = v_bank()
                if b >= 1:
                    dve.wait_ge(g_filled, NT * b)
                split(bank_[:], zT_hi[:], zT_lo[:], v_freed, zT_ready)

            def take_logits(b):
                bank_ = v_bank()
                settle(dve.tensor_tensor(lg[:], bank_[:, 0:TB * E].rearrange("p (n e) -> p n e", n=TB),
                                         gate_b_rows.unsqueeze(1).to_broadcast([P, TB, E]), ALU.add))
                dve.sem_inc(v_freed, 1)
                settle(dve.tensor_tensor(lg2[:], lg[:], lg[:], ALU.mult))
                dve.tensor_reduce(mean_square[:], lg2[:], AX.X, ALU.add).then_inc(square_ready, 1)

            def route(b):
                dve.wait_ge(logits_normed, b + 1)
                settle(dve.tensor_reduce(rt[:, 3, :], lg[:], AX.X, ALU.max))
                dve.tensor_tensor(lg2[:], lg[:], rt[:, 3, :].unsqueeze(2).to_broadcast([P, TB, E]),
                                  ALU.subtract).then_inc(gate_in, 1)

            def take_gates(b):
                dve.wait_ge(gate_exp, b + 1)
                settle(dve.tensor_reduce(rt[:, 0, :], lge[:], AX.X, ALU.add))
                settle(dve.reciprocal(rt[:, 1, :], rt[:, 0, :]))
                settle(dve.tensor_scalar(rt[:, 2, :], rt[:, 1, :], EPS_GATE, None, ALU.add))
                settle(dve.reciprocal(rt[:, 3, :], rt[:, 2, :]))
                settle(dve.tensor_tensor(gate[b % 2][:], rt[:, 1, :], rt[:, 3, :], ALU.mult))

            def take_ffn(b):
                bank_ = v_bank()
                if b >= 1:
                    dve.wait_ge(stored, 16 * b)
                for n in range(TB):
                    ins = dve.scalar_tensor_tensor(out=result[:, n, :], in0=bank_[:, n * P:(n + 1) * P],
                                                   scalar=gate[b % 2][:, n:n + 1], in1=x2[b % 2][:, n, :],
                                                   op0=ALU.mult, op1=ALU.add)
                settle(ins)
                dve.sem_inc(v_freed, 1)
                dve.sem_inc(result_ready, 1)

            def side(b, s, k):
                for stage, of in due(b, s, k, B):
                    if stage == "y_low":
                        take_y(of, 0)
                    if stage == "y_high":
                        take_y(of, 1)
                    if stage == "y_norm":
                        take_yT(of)
                    if stage == "attention":
                        take_attention(of)
                    if stage == "z_norm":
                        normalise_z(of)
                    if stage == "z":
                        take_zT(of)
                    if stage == "logits":
                        take_logits(of)
                    if stage == "route":
                        route(of)
                    if stage == "gates":
                        take_gates(of)
                    if stage == "ffn":
                        take_ffn(of)
                    if stage == "b2" and of == 0:
                        dve.tensor_reduce(b2_sum[:], b2_cols, AX.X, ALU.add).then_inc(b2_ready, 1)
                    if stage == "x_stats":
                        take_x(of)
                    if stage == "x_norm":
                        normalise_x(of)
                    if stage == "x":
                        take_xT(of)
                    if stage == "q":
                        take_q(of)
                    if stage == "k":
                        take_k(of)
                    if stage == "v":
                        take_v(of)

            take_x(0)
            root_x()
            normalise_x(0)
            take_xT(0)
            take_q(0)
            take_k(0)
            take_v(0)
            dve.wait_ge(cst_loaded, 16)
            for k in range(MAX_PLACES):
                max_unit(0, 0, k)
            take_max(0, 0)
            for b in range(B):
                for s in range(SETS):
                    for k in range(PLACES):
                        side(b, s, k)
                        if k < MAX_PLACES:
                            max_unit(*next_set(b, s), k)
                        if k == TAKE_MAX_AT and next_set(b, s)[0] < B:
                            take_max(*next_set(b, s))
            take_y(B - 1, 1)
            take_yT(B - 1)
            take_attention(B - 1)
            root_z(B - 1)
            normalise_z(B - 1)
            take_zT(B - 1)
            take_ffn(B - 2)
            take_logits(B - 1)
            route(B - 1)
            take_gates(B - 1)
            take_ffn(B - 1)


def constants(H, T):
    import numpy as np

    SETS = H // QUADS
    c = np.zeros((P, C_QUAD + QUADS), np.float32)
    c[:, C_IDENT:C_IDENT + P] = np.eye(P)
    c[:, C_MASK + T - P:C_MASK + T] = np.where(np.arange(P)[None, :] > np.arange(P)[:, None], MASKED, 0.0)
    slopes = (2.0 ** (-(8.0 / H) * np.arange(1, H + 1))).astype(np.float32)
    high = (slopes.view(np.uint32) & np.uint32(0xFFFFF000)).view(np.float32)
    c[ALIBI_ROWS:MAX_ROWS, C_KEY:C_KEY + T] = np.arange(T)
    c[MAX_ROWS:MAX_ROWS + 2 * QUADS, C_KEY:C_KEY + T] = 1.0
    for q in range(QUADS):
        heads = slice(QUADS * q, QUADS * q + SETS)
        c[ALIBI_ROWS + q, C_QUERY:C_QUERY + SETS] = high[heads]
        c[ALIBI_ROWS + QUADS + q, C_QUERY:C_QUERY + SETS] = (slopes - high)[heads]
        c[CONST_ROWS + q:P:QUADS, C_QUAD + q] = 1.0
    return c


def qk_order(a):
    import numpy as np

    q, k, v = np.split(a.reshape(-1, 3 * P), 3, 1)
    q = q.reshape(-1, QUADS, 4, 8).swapaxes(-1, -2)
    k = k.reshape(-1, QUADS, 2, 2, 8).swapaxes(-1, -2)
    return np.concatenate([q.reshape(-1, P), k.reshape(-1, P), v], 1).reshape(a.shape)


def kernel(**inputs):
    import numpy as np
    import concourse.bacc as bacc
    from concourse.bass_utils import run_bass_kernel_spmd

    a = {name: np.ascontiguousarray(v) for name, v in inputs.items()}
    x, w1, w2 = a["L0_attn_x"], a["L0_ffn_w1"], a["L0_ffn_w2"]
    E, C, F = w1.shape
    w_attn, b_attn = qk_order(a["L0_attn_w_attn"]), qk_order(a["L0_attn_b_attn"])
    by_tile = lambda v: v.reshape((E * F // P, P) + v.shape[2:]).swapaxes(0, 1)
    arrays = {
        "x": x,
        "w_attn": w_attn,
        "w_proj": a["L0_attn_w_proj"],
        "w1": w1.swapaxes(0, 1).reshape(C, E * F),
        "w2": by_tile(w2),
        "columns": np.concatenate([a["L0_ffn_gate_w"].T, a["L0_ffn_b2"].T, by_tile(a["L0_ffn_b1"]),
                                   b_attn[:2 * C].reshape(2, C).T], 1),
        "rows": np.concatenate([b_attn[2 * C:], a["L0_attn_b_proj"], a["L0_ffn_gate_b"], a["L0_ffn_rms_w"]])[None],
        "consts": constants(16, x.shape[1]),
    }
    arrays = {name: np.ascontiguousarray(v) for name, v in arrays.items()}

    nc = bacc.Bacc("TRN2", target_bir_lowering=False, num_devices=1)
    args = [nc.dram_tensor(name, v.shape, mybir.dt.from_np(v.dtype), kind="ExternalInput").ap()
            for name, v in arrays.items()]
    args.append(nc.dram_tensor("out", x.shape, F32, kind="ExternalOutput").ap())
    block_kernel(nc, *args)
    r = run_bass_kernel_spmd(nc, [arrays], core_ids=[0])
    return r.results[0]["out"]
```

```python
from contextlib import ExitStack

from concourse import mybir

ALU = mybir.AluOpType
ACT = mybir.ActivationFunctionType
AX = mybir.AxisListType
F32 = mybir.dt.float32
F32R = mybir.dt.float32r
BF16 = mybir.dt.bfloat16
I32 = mybir.dt.int32

P = 128
QUADS = 4
QR = P // QUADS
TERMS = 3
MASKED = -3.0e38
MASKED_SCORE = -1.0e30
EPS_LN = 1e-5
EPS_F32 = 1.1920929e-07
EPS_GATE = 1e-6
RSQRT_GUESS = 0x5F3759DF
V_BANKS, A_BANKS = 3, 3
KINDS = 3

CONST_ROWS = 96
ALIBI_ROWS, MAX_ROWS = 96, 104
C_IDENT, C_MASK, C_KEY, C_QUERY, C_QUAD = 0, 128, 640, 1152, 1156


PLACES = 16
EARLY_PLAN = {
    "max": (-1, 0, 2, 3, 4, 5, 6, 8, 8, 9, 11, 11), "take_max": (12,),
    "exp": (4, 4, 5, 6, 8, 8, 9, 11, 11, 13, 14, 14), "pv": (11, 15), "pv_last": (0,),
}
LATER_PLAN = {
    "max": (-1, -1, 2, 3, 4, 5, 6, 7, 8, 9, 10, 11), "take_max": (13,),
    "exp": (4, 5, 6, 7, 8, 9, 10, 10, 12, 13, 14, 15), "pv": (12, 15), "pv_last": (0,),
}
STAGES = {
    "y_low": (2, 14, 0), "y_high": (0, 4, 1), "y_norm": (0, 5, 1), "attention": (0, 7, 1),
    "z_norm": (0, 13, 1), "z": (0, 15, 1), "logits": (2, 4, 1), "route": (2, 13, 1), "gates": (3, 13, 1),
    "ffn": (1, 14, 2), "x_stats": (0, 15, -1), "x_norm": (1, 7, -1), "x": (1, 10, -1), "k": (1, 12, -1),
    "q": (1, 15, -1), "v": (1, 14, -1), "b2": (2, 15, 0),
}
SCALAR_STAGES = {
    "k_high": (1, 7, -1), "q_high": (1, 11, -1), "gates": (3, 1, 1),
}
TILES = (5, 1, 5, 5)
LAST_TILES = (2, 2, 4)
FFN1_AT = (1, 1, 2, 2, 4)
FFN2_AT = (4, 7, 9, 11, 14)
FFN_TAIL_AT, LOGITS_TAIL_AT = 4, 8


def due(stages, b, s, k, batches):
    return [(name, b - behind) for name, (step, place, behind) in stages.items()
            if (s, k) == (step, place) and 0 <= b - behind < batches]


def block_kernel(nc, x, w_attn, w_proj, w1, w2, columns, rows, consts, out):
    B, T, C = x.shape
    H = 16
    D = C // H
    NT = w2.shape[1]
    E = (columns.shape[1] - NT - 2) // 2
    TB = T // P
    SETS = H // QUADS
    UNITS = KINDS * QUADS
    HB = 6
    Q_LOADS = 16 * TERMS
    K_LOADS = 16 * 2
    K_LOW_LOADS = 16
    assert C == P and T == 512 and D == 8 and NT == 16

    MAX_BLOCKS = [[3], [2, 0], [1]]
    KEY_BLOCKS = [[0], [1, 3], [2]]
    KIND_AT = [0, 512, 1024]
    PCOLS = 1280

    with ExitStack() as ctx:
        def sb(name, shape, dt=F32):
            return ctx.enter_context(nc.sbuf_tensor(name, shape, dt))

        def bank(name):
            return ctx.enter_context(nc.psum_tensor(name, [P, 512], F32))

        def sem(name):
            return ctx.enter_context(nc.semaphore(name))

        cst = sb("cst", [P, C_QUAD + QUADS])
        ident = cst[:, C_IDENT:C_IDENT + P]
        zeros = sb("zeros", [P, T])
        ident_bf = sb("ident_bf", [P, P], BF16)
        score_mask = sb("score_mask", [P, P], BF16)
        w_attn_sb = sb("w_attn_sb", [P, 3 * C])
        w_attn_hi = sb("w_attn_hi", [P, 3 * C], F32R)
        w_attn_lo = sb("w_attn_lo", [P, 3 * C], F32R)
        w_proj_sb = sb("w_proj_sb", [P, C])
        w1_hi = sb("w1_hi", [P, NT * P], F32R)
        w1_lo = sb("w1_lo", [P, NT * P], F32R)
        w2_sb = sb("w2_sb", [P, NT, C])
        cols_sb = sb("cols_sb", [P, 2 * E + NT + 2])
        gate_sb = cols_sb[:, 0:E]
        b2_cols = cols_sb[:, E:2 * E]
        b1_cols = cols_sb[:, 2 * E:2 * E + NT]
        bq = cols_sb[:, 2 * E + NT:2 * E + NT + 1]
        bk = cols_sb[:, 2 * E + NT + 1:2 * E + NT + 2]
        gate_parts = sb("gate_parts", [P, 2 * E], F32R)
        rows_sb = sb("rows_sb", [P, 2 * C + 2 * E])
        bv_rows = rows_sb[:, 0:C]
        b_proj_rows = rows_sb[:, C:2 * C]
        gate_b_rows = rows_sb[:, 2 * C:2 * C + E]
        rms_rows = rows_sb[:, 2 * C + E:2 * C + 2 * E]
        b2_sum = sb("b2_sum", [P, 1])

        x_in = sb("x_in", [P, TB, C])
        stats1 = sb("stats1", [P, TB, 6])
        mv1 = sb("mv1", [P, TB, 2])
        rstd1 = sb("rstd1", [P, TB])
        xn = sb("xn", [P, TB, C])
        xT_hi = sb("xT_hi", [P, T], F32R)
        xT_lo = sb("xT_lo", [P, T], F32R)
        q_full = sb("q_full", [P, T])
        k_full = sb("k_full", [P, T])
        q_hi = sb("q_hi", [P, T], F32R)
        q_lo = sb("q_lo", [P, T], F32R)
        k_hi = sb("k_hi", [P, T], F32R)
        k_lo = sb("k_lo", [P, T], F32R)
        q_stack = [sb(f"q_stack{i}", [P, SETS, T], F32R) for i in range(2)]
        k_stack = sb("k_stack", [P, SETS, QUADS, T], F32R)
        v_ones = [sb(f"v_ones{i}", [P, TB, SETS, QUADS, QR]) for i in range(2)]

        row_max = sb("row_max", [P, 2, TB * QUADS])
        unused = sb("unused", [P, V_BANKS, T], BF16)
        m_hi = sb("m_hi", [TB * QUADS, P], F32R)
        m_lo = sb("m_lo", [TB * QUADS, P], F32R)
        probs = sb("probs", [P, 2, QUADS, PCOLS])
        y_raw = sb("y_raw", [P, 2, T])
        rden = sb("rden", [P, 2, TB * QUADS, 2])
        y_norm = sb("y_norm", [P, TB * C])
        yT = sb("yT", [P, T])

        x_res = sb("x_res", [P, TB, C])
        xb_res = sb("xb_res", [P, TB, C])
        x2 = [sb(f"x2_{i}", [P, TB, C]) for i in range(2)]
        stats2 = sb("stats2", [P, TB, 6])
        mv2 = sb("mv2", [P, TB, 2])
        rstd2 = sb("rstd2", [P, TB])
        z = sb("z", [P, TB, C])
        zT_hi = sb("zT_hi", [P, T], F32R)
        zT_lo = sb("zT_lo", [P, T], F32R)
        var = sb("var", [P, 2, TB])
        mean_square = sb("mean_square", [P, TB])
        inverse_rms = sb("inverse_rms", [P, TB])
        lg = sb("lg", [P, TB, E])
        lg2 = sb("lg2", [P, TB, E])
        lge = sb("lge", [P, TB, E])
        rt = sb("rt", [P, 4, TB])
        gate = [sb(f"gate{i}", [P, TB]) for i in range(2)]
        hidden = sb("hidden", [P, HB, T])
        w1_sb = hidden[:, 0:NT * P // T, :].rearrange("p n t -> p (n t)")
        ffn_T = sb("ffn_T", [P, T])
        result = sb("result", [P, TB, C])

        v_ring = [bank(f"v_ring{i}") for i in range(V_BANKS)]
        a_ring = [bank(f"a_ring{i}") for i in range(A_BANKS)]
        pv_bank = bank("pv_bank")
        ffn_bank = bank("ffn_bank")

        x_loaded = sem("x_loaded")
        cst_loaded = sem("cst_loaded")
        wa_loaded = sem("wa_loaded")
        rows_loaded = sem("rows_loaded")
        wp_loaded = sem("wp_loaded")
        w1_loaded = sem("w1_loaded")
        w2_loaded = sem("w2_loaded")
        xres_loaded = sem("xres_loaded")
        q_loaded = sem("q_loaded")
        k_loaded = [[sem(f"k_loaded{half}{q}") for q in range(QUADS)] for half in range(2)]
        k_low_loaded = [[sem(f"k_low_loaded{half}{q}") for q in range(QUADS)] for half in range(2)]
        m_loaded = sem("m_loaded")
        stored = sem("stored")
        wa_split = sem("wa_split")
        w1_split = sem("w1_split")
        v_const = sem("v_const")
        zeros_set = sem("zeros_set")
        mask_ready = sem("mask_ready")
        q_const = sem("q_const")
        k_zeros = sem("k_zeros")
        k_const = sem("k_const")
        v_filled = sem("v_filled")
        v_freed = sem("v_freed")
        e_filled = sem("e_filled")
        e_freed = sem("e_freed")
        g_filled = sem("g_filled")
        g_freed = sem("g_freed")
        dve_step = sem("dve_step")
        xn_ready = sem("xn_ready")
        xT_ready = sem("xT_ready")
        q_ready = sem("q_ready")
        k_ready = sem("k_ready")
        q_split = sem("q_split")
        k_split = sem("k_split")
        pool_step = sem("pool_step")
        v_ready = sem("v_ready")
        max_ready = sem("max_ready")
        m_ready = sem("m_ready")
        pv_done = sem("pv_done")
        pv_evacuated = sem("pv_evacuated")
        y_norm_ready = sem("y_norm_ready")
        yT_ready = sem("yT_ready")
        xb_ready = sem("xb_ready")
        x_stats_ready = sem("x_stats_ready")
        z_stats_ready = sem("z_stats_ready")
        x_rstd_ready = sem("x_rstd_ready")
        z_rstd_ready = sem("z_rstd_ready")
        square_ready = sem("square_ready")
        logits_normed = sem("logits_normed")
        z_ready = sem("z_ready")
        zT_ready = sem("zT_ready")
        x2_ready = sem("x2_ready")
        gate_in = sem("gate_in")
        gate_exp = sem("gate_exp")
        ffn2_done = sem("ffn2_done")
        b2_ready = sem("b2_ready")
        ffn_evacuated = sem("ffn_evacuated")
        result_ready = sem("result_ready")

        x_view = x.rearrange("b (n p) c -> b p n c", p=P)
        out_view = out.rearrange("b (n p) c -> b p n c", p=P)

        def q_count(b):
            return Q_LOADS * b + 16 * max(0, b - 2)

        def next_set(b, s):
            return (b, s + 1) if s < SETS - 1 else (b + 1, 0)

        def plan(n):
            return EARLY_PLAN if n <= SETS else LATER_PLAN

        def planned(b, s, k, what):
            return [unit for unit, place in enumerate(plan(SETS * b + s)[what]) if place == k]

        def maxima_due(n, k):
            units = []
            for ahead in (1, 2):
                for unit, place in enumerate(plan(n + ahead - 1)["max"]):
                    at = place if (n + ahead) % SETS else max(place, 0)
                    if at == k - PLACES * (ahead - 1) and n + ahead < SETS * B:
                        units.append(((n + ahead) // SETS, (n + ahead) % SETS, unit))
            return units

        def chunk(b, s):
            n = SETS * b + s - SETS - 1
            if n < 0:
                return 0, range(0)
            sizes = LAST_TILES if b == B - 1 and s > 0 else TILES
            first = sum(sizes[:n % SETS])
            return n // SETS, range(first, first + sizes[n % SETS])

        def send_k(queue, part, half, g, q, loaded):
            rows = QR * q + half * QR // 2
            queue.dma_start(k_stack[QR * g + q * D:QR * g + (q + 1) * D, 2 * half:2 * half + 2, q, :].bitcast(F32),
                            part[rows:rows + QR // 2, :].bitcast(F32)).then_inc(loaded, 16)

        def inverse_sqrt(engine, settle, y, src, scale, eps, v, t, fused=False):
            settle(engine.tensor_scalar(v, src, scale, eps, ALU.mult, ALU.add))
            settle(engine.tensor_scalar(y.bitcast(I32), v.bitcast(I32), -0.5, float(RSQRT_GUESS), ALU.mult, ALU.add))
            for _ in range(3):
                if fused:
                    settle(engine.scalar_tensor_tensor(out=t, in0=y, scalar=-0.5, in1=y, op0=ALU.mult, op1=ALU.mult))
                    settle(engine.tensor_tensor(t, t, v, ALU.mult))
                    settle(engine.scalar_tensor_tensor(out=y, in0=t, scalar=1.5, in1=y, op0=ALU.add, op1=ALU.mult))
                else:
                    settle(engine.tensor_tensor(t, y, y, ALU.mult))
                    settle(engine.tensor_tensor(t, t, v, ALU.mult))
                    settle(engine.tensor_scalar(t, t, -0.5, 1.5, ALU.mult, ALU.add))
                    settle(engine.tensor_tensor(y, y, t, ALU.mult))

        block = ctx.enter_context(nc.Block())

        @block.sync
        def _(sp):
            def load_x(b):
                if b >= 1:
                    sp.wait_ge(xn_ready, b)
                sp.dma_start(x_in[:], x_view[b]).then_inc(x_loaded, 16)

            def load_residual(b):
                if b >= 1:
                    sp.wait_ge(xb_ready, b)
                sp.dma_start(x_res[:], x_view[b]).then_inc(xres_loaded, 16)

            def load_q(b):
                if b >= 2:
                    sp.wait_ge(e_filled, UNITS * SETS * (b - 1))
                    sp.dma_start(q_stack[b % 2][MAX_ROWS:MAX_ROWS + 2 * QUADS, :, :].bitcast(F32),
                                 zeros[0:2 * QUADS * SETS, :]).then_inc(q_loaded, 16)
                for g, part in ((0, 0), (1, 0), (2, 1)):
                    sp.wait_ge(q_split, 2 * b + part + 1)
                    sp.dma_start(q_stack[b % 2][QR * g:QR * (g + 1), :, :].bitcast(F32),
                                 (q_hi, q_lo)[part][:].bitcast(F32)).then_inc(q_loaded, 16)

            def load_k(b, half):
                if b == 0:
                    sp.wait_ge(k_zeros, half + 1)
                else:
                    sp.wait_ge(e_filled, UNITS * (SETS * (b - 1) + 2 * half + 2))
                sp.wait_ge(k_split, 2 * b + 1)
                for q in range(QUADS):
                    for g in (0, 2):
                        send_k(sp, k_hi, half, g, q, k_loaded[half][q])

            def load_max(b, s):
                sp.wait_ge(m_ready, SETS * b + s + 1)
                for r, part in ((MAX_ROWS, m_hi), (MAX_ROWS + QUADS, m_lo)):
                    sp.dma_start(q_stack[b % 2][r:r + QUADS, s, :].bitcast(F32),
                                 part[:].bitcast(F32)).then_inc(m_loaded, 16)

            def store(b):
                sp.wait_ge(result_ready, b + 1)
                sp.dma_start(out_view[b], result[:]).then_inc(stored, 16)

            load_x(0)
            sp.dma_start(w_attn_sb[:], w_attn).then_inc(wa_loaded, 16)
            sp.dma_start(cst[:], consts).then_inc(cst_loaded, 16)
            sp.dma_start(cols_sb[:], columns).then_inc(rows_loaded, 16)
            sp.dma_start(rows_sb[:], rows.to_broadcast([P, rows.shape[1]])).then_inc(rows_loaded, 16)
            sp.dma_start(w1_sb[:], w1).then_inc(w1_loaded, 16)
            load_q(0)
            load_k(0, 0)
            load_k(0, 1)
            sp.dma_start(w_proj_sb[:], w_proj).then_inc(wp_loaded, 16)
            sp.dma_start(w2_sb[:], w2).then_inc(w2_loaded, 16)
            load_residual(0)
            load_x(1)
            load_max(0, 0)
            for b in range(B):
                for s in range(SETS):
                    if s == 0 and b >= 1:
                        load_k(b, 1)
                        load_residual(b)
                        if b + 1 < B:
                            load_x(b + 1)
                    if s == 1 and b >= 2:
                        store(b - 2)
                    if s == 2 and b + 1 < B:
                        load_k(b + 1, 0)
                        load_q(b + 1)
                    if next_set(b, s)[0] < B:
                        load_max(*next_set(b, s))
            store(B - 2)
            store(B - 1)
            sp.wait_ge(stored, 16 * B)

        @block.gpsimd
        def _(pool):
            def split(src, hi, lo, done, step):
                pool.tensor_copy(hi, src).then_inc(done, 1)
                pool.wait_ge(done, step + 1)
                pool.tensor_tensor(lo, src, hi.bitcast(F32), ALU.subtract).then_inc(done, 1)

            def split_low(b, part):
                full, hi, lo, parts, loads, count = (
                    (k_full, k_hi, k_lo, k_split, k_low_loaded[0] + k_low_loaded[1], K_LOW_LOADS * b),
                    (q_full, q_hi, q_lo, q_split, [q_loaded], q_count(b)))[part]
                pool.wait_ge(parts, 2 * b + 1)
                if b >= 1:
                    for loaded in loads:
                        pool.wait_ge(loaded, count)
                pool.tensor_tensor(lo[:], full[:], hi[:].bitcast(F32), ALU.subtract).then_inc(parts, 1)

            def set_ones(tile, e):
                slots = tile[:].rearrange("p n (s e) q i -> p (n s) e q i", e=2)[:, :, e, :, :]
                pool.memset(slots[:, :, :, 16 + 8 * e:24 + 8 * e], 1.0).then_inc(v_const, 1)

            def load_k_low(b, half):
                if b == 0:
                    pool.wait_ge(k_zeros, half + 1)
                else:
                    pool.wait_ge(e_filled, UNITS * (SETS * (b - 1) + 2 * half + 2))
                pool.wait_ge(k_split, 2 * b + 2)
                for q in range(QUADS):
                    send_k(pool, k_lo, half, 1, q, k_low_loaded[half][q])

            steps = [0]

            def settle(ins):
                steps[0] += 1
                ins.then_inc(pool_step, 1)
                pool.wait_ge(pool_step, steps[0])

            def x_rstd(b):
                pool.wait_ge(x_stats_ready, b + 1)
                inverse_sqrt(pool, settle, rstd1[:], mv1[:, :, 1], 1.0, EPS_LN, var[:, 0, :], var[:, 1, :])
                pool.sem_inc(x_rstd_ready, 1)

            def z_rstd(b):
                pool.wait_ge(z_stats_ready, b + 1)
                inverse_sqrt(pool, settle, rstd2[:], mv2[:, :, 1], 1.0, EPS_LN, var[:, 0, :], var[:, 1, :])
                pool.sem_inc(z_rstd_ready, 1)

            def norm_logits(b):
                pool.wait_ge(square_ready, b + 1)
                inverse_sqrt(pool, settle, inverse_rms[:], mean_square[:], 1.0 / E, EPS_F32, var[:, 0, :], var[:, 1, :])
                settle(pool.tensor_tensor(lg2[:], lg[:], inverse_rms[:].unsqueeze(2).to_broadcast([P, TB, E]), ALU.mult))
                pool.tensor_tensor(lg[:], lg2[:], rms_rows.unsqueeze(1).to_broadcast([P, TB, E]),
                                   ALU.mult).then_inc(logits_normed, 1)

            pool.memset(zeros[:], 0.0).then_inc(zeros_set, 1)
            pool.wait_ge(zeros_set, 1)
            pool.affine_select(out=ident_bf[:], in_=zeros[:, 0:P], compare_op=ALU.not_equal, fill=1.0, base=0,
                               pattern=[[1, P]], channel_multiplier=-1).then_inc(mask_ready, 1)
            pool.affine_select(out=score_mask[:], in_=zeros[:, 0:P], compare_op=ALU.is_ge, fill=MASKED_SCORE, base=0,
                               pattern=[[1, P]], channel_multiplier=-1).then_inc(mask_ready, 1)
            pool.memset(k_stack[0:CONST_ROWS, 0:2, :, :].bitcast(F32), 0.0).then_inc(k_zeros, 1)
            pool.wait_ge(wa_loaded, 16)
            split(w_attn_sb[:], w_attn_hi[:], w_attn_lo[:], wa_split, 0)
            settle(pool.memset(v_ones[0][:], 0.0))
            for e in range(2):
                set_ones(v_ones[0], e)
            pool.memset(k_stack[0:CONST_ROWS, 2:4, :, :].bitcast(F32), 0.0).then_inc(k_zeros, 1)
            split_low(0, 1)
            split_low(0, 0)
            load_k_low(0, 0)
            load_k_low(0, 1)
            settle(pool.memset(v_ones[1][:], 0.0))
            for e in range(2):
                set_ones(v_ones[1], e)

            def residual(b):
                pool.wait_ge(xres_loaded, 16 * (b + 1))
                if b >= 1:
                    pool.wait_ge(x2_ready, b)
                pool.tensor_tensor(xb_res[:], x_res[:], b_proj_rows.unsqueeze(1).to_broadcast([P, TB, C]),
                                   ALU.add).then_inc(xb_ready, 1)

            for b in range(B):
                for s in range(SETS):
                    if s == 0 and b >= 1:
                        load_k_low(b, 1)
                        z_rstd(b - 1)
                    if s == 1 and b + 1 < B:
                        x_rstd(b + 1)
                        split_low(b + 1, 0)
                        split_low(b + 1, 1)
                    if s == 1 and b >= 1:
                        norm_logits(b - 1)
                    if s == 2 and b + 1 < B:
                        load_k_low(b + 1, 0)
                    if b == 0 and s == 0:
                        pool.wait_ge(w1_loaded, 16)
                        split(w1_sb[:], w1_hi[:], w1_lo[:], w1_split, 0)
                        pool.wait_ge(rows_loaded, 32)
                        split(gate_sb, gate_parts[:, 0:E], gate_parts[:, E:2 * E], w1_split, 2)
                    if s == 2:
                        residual(b)
            norm_logits(B - 1)

        @block.scalar
        def _(act):
            uses = [0]

            def a_bank():
                uses[0] += 1
                return a_ring[(uses[0] - 1) % A_BANKS]

            def exp_unit(b, s, kind, q):
                n = SETS * b + s
                unit = UNITS * n + QUADS * kind + q
                act.wait_ge(e_filled, unit + 1)
                if n >= 2 and kind == 0 and q == 0:
                    act.wait_ge(pv_done, n - 1)
                cols = 128 * sum(TB - j for j in KEY_BLOCKS[kind])
                act.activation(probs[:, n % 2, q, KIND_AT[kind]:KIND_AT[kind] + cols],
                               a_bank()[:, 0:cols], ACT.Exp).then_inc(e_freed, 1)

            def evacuate_pv(b, half):
                act.wait_ge(pv_done, SETS * b + 2 * half + 2)
                if b >= 1:
                    act.wait_ge(y_norm_ready, 2 * (b - 1) + half + 1)
                act.activation(y_raw[:, half, :], pv_bank[:], ACT.Copy).then_inc(pv_evacuated, 1)

            def gelu_tile(b, m):
                n = NT * b + m
                act.wait_ge(g_filled, n + 1)
                if b == 0 and m == 0:
                    act.wait_ge(rows_loaded, 32)
                    act.wait_ge(w1_split, 2)
                if n >= HB:
                    act.wait_ge(ffn2_done, n - HB + 1)
                act.activation(hidden[:, n % HB, :], a_bank()[:], ACT.Gelu,
                               bias=b1_cols[:, m:m + 1]).then_inc(g_freed, 1)

            def evacuate_ffn(b):
                act.wait_ge(ffn2_done, NT * (b + 1))
                if b == 0:
                    act.wait_ge(b2_ready, 1)
                else:
                    act.wait_ge(result_ready, b)
                act.activation(ffn_T[:], ffn_bank[:], ACT.Identity, bias=b2_sum[:, 0:1]).then_inc(ffn_evacuated, 1)

            def gate_exponentials(b):
                act.wait_ge(gate_in, b + 1)
                act.activation(lge[:], lg2[:], ACT.Exp, scale=2.0).then_inc(gate_exp, 1)

            def split_high(b, part):
                full, hi, ready, parts, loads, count = (
                    (k_full, k_hi, k_ready, k_split, k_loaded[0] + k_loaded[1], K_LOADS * b),
                    (q_full, q_hi, q_ready, q_split, [q_loaded], q_count(b)))[part]
                act.wait_ge(ready, b + 1)
                if b >= 1:
                    for loaded in loads:
                        act.wait_ge(loaded, count)
                act.activation(hi[:], full[:], ACT.Copy).then_inc(parts, 1)

            def q_constants(i):
                for s in range(SETS):
                    act.activation(q_stack[i][CONST_ROWS:P, s, :], zeros[CONST_ROWS:P, :], ACT.Identity,
                                   bias=cst[CONST_ROWS:P, C_QUERY + s:C_QUERY + s + 1]).then_inc(q_const, 1)

            def k_constants(half):
                for q in range(QUADS):
                    act.activation(k_stack[CONST_ROWS:P, 2 * half:2 * half + 2, q, :],
                                   cst[CONST_ROWS:P, C_KEY:C_KEY + T].unsqueeze(1).to_broadcast([QR, 2, T]),
                                   ACT.Copy, scale=cst[CONST_ROWS:P, C_QUAD + q:C_QUAD + q + 1]).then_inc(k_const, 1)

            act.wait_ge(zeros_set, 1)
            act.wait_ge(cst_loaded, 16)
            q_constants(0)
            k_constants(0)
            split_high(0, 1)
            split_high(0, 0)
            k_constants(1)
            q_constants(1)
            for b in range(B):
                for s in range(SETS):
                    if s == 1 and b >= 2:
                        evacuate_ffn(b - 2)
                    fb, tiles = chunk(b, s)
                    for i, m in enumerate(tiles):
                        if s == 0 and i == 2:
                            evacuate_pv(b - 1, 1)
                        gelu_tile(fb, m)
                    if s == 0 and b >= 1 and not tiles:
                        evacuate_pv(b - 1, 1)
                    if s == 2:
                        evacuate_pv(b, 0)
                    for unit in range(UNITS):
                        exp_unit(b, s, unit // QUADS, unit % QUADS)
                        for stage, of in due(SCALAR_STAGES, b, s, unit, B):
                            if stage == "gates":
                                gate_exponentials(of)
                            if stage == "k_high" and of >= 1:
                                split_high(of, 0)
                            if stage == "q_high" and of >= 1:
                                split_high(of, 1)
            evacuate_pv(B - 1, 1)
            for m in range(sum(LAST_TILES), NT):
                gelu_tile(B - 2, m)
            for m in range(NT):
                gelu_tile(B - 1, m)
                if m == 1:
                    evacuate_ffn(B - 2)
                if m == NT - 3:
                    gate_exponentials(B - 1)
            evacuate_ffn(B - 1)

        @block.tensor
        def _(pe):
            uses = [0]
            a_uses = []

            def v_bank():
                n = uses[0]
                uses[0] += 1
                if n >= V_BANKS:
                    pe.wait_ge(v_freed, n - V_BANKS + 1)
                return v_ring[n % V_BANKS]

            def a_bank(freed, count):
                n = len(a_uses)
                a_uses.append((freed, count))
                if n >= A_BANKS:
                    pe.wait_ge(*a_uses[n - A_BANKS])
                return a_ring[n % A_BANKS]

            def split_product(dst, lhs, rhs):
                pe.matmul(dst, lhs[0], rhs[0], start=True, stop=False)
                pe.matmul(dst, lhs[0], rhs[1], start=False, stop=False)
                return pe.matmul(dst, lhs[1], rhs[0], start=False, stop=True)

            def transpose_x(b):
                pe.wait_ge(xn_ready, b + 1)
                if b == 0:
                    pe.wait_ge(cst_loaded, 16)
                dst = v_bank()
                for n in range(TB):
                    last = pe.transpose(dst[:, n * P:(n + 1) * P], xn[:, n, :], ident)
                last.then_inc(v_filled, 1)

            def project_qk(b, part):
                pe.wait_ge(xT_ready, b + 1)
                if b == 0:
                    pe.wait_ge(wa_split, 2)
                cols = slice(part * C, (part + 1) * C)
                dst = v_bank()
                split_product(dst[:], (w_attn_hi[:, cols], w_attn_lo[:, cols]),
                              (xT_hi[:], xT_lo[:])).then_inc(v_filled, 1)

            def project_v(b):
                cols = slice(2 * C, 3 * C)
                dst = v_bank()
                for n in range(TB):
                    tok = slice(n * P, (n + 1) * P)
                    last = split_product(dst[:, tok], (xT_hi[:, tok], xT_lo[:, tok]),
                                         (w_attn_hi[:, cols], w_attn_lo[:, cols]))
                last.then_inc(v_filled, 1)

            def max_unit(b, s, k):
                if k == 0 and b < 2 and s == 0:
                    pe.wait_ge(q_const, SETS * (b + 1))
                if k == 0 and b == 0 and s % 2 == 0:
                    pe.wait_ge(k_const, QUADS * (s // 2 + 1))
                if k == 0:
                    pe.wait_ge(q_loaded, q_count(b + 1))
                q, kind = k // KINDS, k % KINDS
                if kind == 0 and s % 2 == 0:
                    pe.wait_ge(k_loaded[s // 2][q], K_LOADS * (b + 1))
                    pe.wait_ge(k_low_loaded[s // 2][q], K_LOW_LOADS * (b + 1))
                dst = v_bank()
                at = 0
                for n in MAX_BLOCKS[kind]:
                    last = pe.matmul(dst[:, at:at + P * (n + 1)], q_stack[b % 2][:, s, n * P:(n + 1) * P],
                                     k_stack[:, s, q, 0:P * (n + 1)], start=True, stop=True)
                    at += P * (n + 1)
                last.then_inc(v_filled, 1)

            def transpose_max(b, s):
                n = SETS * b + s
                pe.wait_ge(max_ready, n + 1)
                dst = v_bank()
                pe.transpose(dst[0:TB * QUADS, 0:P], row_max[:, n % 2, :], ident).then_inc(v_filled, 1)

            def exp_unit(b, s, k):
                n = SETS * b + s
                kind, q = k // QUADS, k % QUADS
                if n == 0 and k == 0:
                    pe.wait_ge(mask_ready, 2)
                if k == 0:
                    pe.wait_ge(m_loaded, 32 * (n + 1))
                dst = a_bank(e_freed, UNITS * n + k + 1)
                at = 0
                for j in KEY_BLOCKS[kind]:
                    pe.matmul(dst[:, at:at + P * (TB - j)], k_stack[:, s, q, j * P:(j + 1) * P],
                              q_stack[b % 2][:, s, j * P:T], start=(at == 0), stop=False, skip_group_check=True)
                    at += P * (TB - j)
                blocks = len(KEY_BLOCKS[kind])
                diagonal = dst[:].rearrange("p (a t) -> p a t", t=P)[:, 0::3, :][:, 0:blocks, :]
                pe.matmul(diagonal, ident_bf[:], score_mask[:].unsqueeze(1).to_broadcast([P, blocks, P]),
                          start=False, stop=True, skip_group_check=True).then_inc(e_filled, 1)

            def pv(b, s, kind):
                n = SETS * b + s
                pe.wait_ge(e_freed, UNITS * n + QUADS * (kind + 1))
                if kind == 0 and s == 0:
                    pe.wait_ge(v_ready, b + 1)
                    if b == 0:
                        pe.wait_ge(v_const, 2)
                    if b == 1:
                        pe.wait_ge(v_const, 4)
                if kind == 0 and s % 2 == 0 and n >= 2:
                    pe.wait_ge(pv_evacuated, n // 2)
                at = KIND_AT[kind]
                for j in KEY_BLOCKS[kind]:
                    cols = P * (TB - j)
                    for q in range(QUADS):
                        last = pe.matmul(pv_bank[QR * q:QR * (q + 1), j * P:T], v_ones[b % 2][:, j, s, q, :],
                                         probs[:, n % 2, q, at:at + cols],
                                         start=(s % 2 == 0 and j == 0), stop=(s % 2 == 1 and j == 2),
                                         tile_position=(0, QR * q), skip_group_check=True)
                    at += cols
                if kind == KINDS - 1:
                    last.then_inc(pv_done, 1)

            def transpose_y(b, half):
                pe.wait_ge(pv_evacuated, 2 * b + half + 1)
                dst = v_bank()
                for n in range(TB):
                    last = pe.transpose(dst[:, n * P:(n + 1) * P], y_raw[:, half, n * P:(n + 1) * P], ident)
                last.then_inc(v_filled, 1)

            def transpose_y_norm(b):
                pe.wait_ge(y_norm_ready, 2 * (b + 1))
                dst = v_bank()
                for n in range(TB):
                    last = pe.transpose(dst[:, n * P:(n + 1) * P], y_norm[:, n * P:(n + 1) * P], ident)
                last.then_inc(v_filled, 1)

            def project_y(b):
                pe.wait_ge(yT_ready, b + 1)
                if b == 0:
                    pe.wait_ge(wp_loaded, 16)
                dst = v_bank()
                for n in range(TB):
                    last = pe.matmul(dst[:, n * P:(n + 1) * P], yT[:, n * P:(n + 1) * P], w_proj_sb[:],
                                     start=True, stop=True)
                last.then_inc(v_filled, 1)

            def transpose_z(b):
                pe.wait_ge(z_ready, b + 1)
                dst = v_bank()
                for n in range(TB):
                    last = pe.transpose(dst[:, n * P:(n + 1) * P], z[:, n, :], ident)
                last.then_inc(v_filled, 1)

            def logits(b):
                pe.wait_ge(zT_ready, b + 1)
                if b == 0:
                    pe.wait_ge(w1_split, 4)
                dst = v_bank()
                for n in range(TB):
                    tok = slice(n * P, (n + 1) * P)
                    sums = dst[:, 2 * n * E:2 * (n + 1) * E]
                    pe.matmul(sums, zT_hi[:, tok], gate_parts[:], start=True, stop=False)
                    last = pe.matmul(sums, zT_lo[:, tok], gate_parts[:], start=False, stop=True)
                last.then_inc(v_filled, 1)

            def ffn1(b, m):
                n = NT * b + m
                if m == 0:
                    pe.wait_ge(zT_ready, b + 1)
                dst = a_bank(g_freed, n + 1)
                cols = slice(m * P, (m + 1) * P)
                split_product(dst[:], (w1_hi[:, cols], w1_lo[:, cols]), (zT_hi[:], zT_lo[:])).then_inc(g_filled, 1)

            def ffn2(b, m):
                n = NT * b + m
                pe.wait_ge(g_freed, n + 1)
                if b == 0 and m == 0:
                    pe.wait_ge(w2_loaded, 16)
                if b >= 1 and m == 0:
                    pe.wait_ge(ffn_evacuated, b)
                pe.matmul(ffn_bank[:], w2_sb[:, m, :], hidden[:, n % HB, :], start=(m == 0),
                          stop=(m == NT - 1)).then_inc(ffn2_done, 1)

            def transpose_ffn(b):
                pe.wait_ge(ffn_evacuated, b + 1)
                dst = v_bank()
                for n in range(TB):
                    last = pe.transpose(dst[:, n * P:(n + 1) * P], ffn_T[:, n * P:(n + 1) * P], ident)
                last.then_inc(v_filled, 1)

            def side(b, s, k):
                for stage, of in due(STAGES, b, s, k, B):
                    if stage == "y_low":
                        transpose_y(of, 0)
                    if stage == "y_high":
                        transpose_y(of, 1)
                    if stage == "y_norm":
                        transpose_y_norm(of)
                    if stage == "attention":
                        project_y(of)
                    if stage == "z":
                        transpose_z(of)
                    if stage == "logits":
                        logits(of)
                    if stage == "ffn":
                        transpose_ffn(of)
                    if stage == "x":
                        transpose_x(of)
                    if stage == "q":
                        project_qk(of, 0)
                    if stage == "k":
                        project_qk(of, 1)
                    if stage == "v":
                        project_v(of)
                fb, tiles = chunk(b, s)
                for m, at in zip(tiles, FFN1_AT):
                    if k == at:
                        ffn1(fb, m)
                for m, at in zip(tiles, FFN2_AT):
                    if k == at:
                        ffn2(fb, m)

            transpose_x(0)
            project_qk(0, 0)
            project_qk(0, 1)
            project_v(0)
            for k in range(UNITS):
                max_unit(0, 0, k)
            transpose_max(0, 0)
            for k in range(PLACES):
                for unit in maxima_due(-1, k):
                    if unit[1] == 1:
                        max_unit(*unit)
            for b in range(B):
                for s in range(SETS):
                    n = SETS * b + s
                    for k in range(PLACES):
                        side(b, s, k)
                        for unit in maxima_due(SETS * b + s, k):
                            max_unit(*unit)
                        if planned(b, s, k, "take_max") and next_set(b, s)[0] < B:
                            transpose_max(*next_set(b, s))
                        for unit in planned(b, s, k, "exp"):
                            exp_unit(b, s, unit)
                        for kind in planned(b, s, k, "pv"):
                            pv(b, s, kind)
                        if planned(b, s, k, "pv_last") and n >= 1:
                            pv((n - 1) // SETS, (n - 1) % SETS, KINDS - 1)
            pv(B - 1, SETS - 1, KINDS - 1)
            tiles = range(sum(LAST_TILES), NT)
            for i, m in enumerate(tiles):
                ffn1(B - 2, m)
                if i >= 2:
                    ffn2(B - 2, m - 2)
                if i == 1:
                    transpose_y(B - 1, 1)
                if i == 2:
                    transpose_y_norm(B - 1)
                if i == 3:
                    project_y(B - 1)
            ffn2(B - 2, NT - 2)
            transpose_z(B - 1)
            ffn2(B - 2, NT - 1)
            for m in range(NT + 2):
                if m < NT:
                    ffn1(B - 1, m)
                if m == FFN_TAIL_AT:
                    transpose_ffn(B - 2)
                if m >= 2:
                    ffn2(B - 1, m - 2)
                if m == LOGITS_TAIL_AT:
                    logits(B - 1)
            transpose_ffn(B - 1)

        @block.vector
        def _(dve):
            uses = [0]
            steps = [0]

            def v_bank():
                uses[0] += 1
                dve.wait_ge(v_filled, uses[0])
                return v_ring[(uses[0] - 1) % V_BANKS]

            def settle(ins):
                steps[0] += 1
                ins.then_inc(dve_step, 1)
                dve.wait_ge(dve_step, steps[0])

            def split(src, hi, lo, freed, ready):
                settle(dve.tensor_copy(hi, src))
                settle(dve.tensor_tensor(lo, src, hi.bitcast(F32), ALU.subtract))
                dve.sem_inc(freed, 1)
                dve.sem_inc(ready, 1)

            def statistics(src, stats, mv, ready):
                for n in range(TB):
                    ins = dve.bn_stats(stats[:, n, :], src[:, n, :])
                settle(ins)
                for n in range(TB):
                    ins = dve.bn_aggr(mv[:, n, :], stats[:, n, :])
                ins.then_inc(ready, 1)

            def normalise(src, mv, rstd, dst, ready):
                for n in range(TB):
                    ins = dve.tensor_scalar(dst[:, n, :], src[:, n, :], mv[:, n, 0:1], rstd[:, n:n + 1],
                                            ALU.subtract, ALU.mult)
                ins.then_inc(ready, 1)

            def take_x(b):
                dve.wait_ge(x_loaded, 16 * (b + 1))
                if b >= 1:
                    dve.wait_ge(xn_ready, b)
                statistics(x_in, stats1, mv1, x_stats_ready)

            def root_x():
                dve.wait_ge(x_stats_ready, 1)
                inverse_sqrt(dve, settle, rstd1[:], mv1[:, :, 1], 1.0, EPS_LN, rt[:, 0, :], rt[:, 1, :], fused=True)
                dve.sem_inc(x_rstd_ready, 1)

            def root_z(b):
                dve.wait_ge(z_stats_ready, b + 1)
                inverse_sqrt(dve, settle, rstd2[:], mv2[:, :, 1], 1.0, EPS_LN, rt[:, 0, :], rt[:, 1, :], fused=True)
                dve.sem_inc(z_rstd_ready, 1)

            def normalise_x(b):
                dve.wait_ge(x_stats_ready, b + 1)
                dve.wait_ge(x_rstd_ready, b + 1)
                if b >= 1:
                    dve.wait_ge(xT_ready, b)
                normalise(x_in, mv1, rstd1, xn, xn_ready)

            def normalise_z(b):
                dve.wait_ge(z_stats_ready, b + 1)
                dve.wait_ge(z_rstd_ready, b + 1)
                normalise(x2[b % 2], mv2, rstd2, z, z_ready)

            def take_xT(b):
                bank_ = v_bank()
                split(bank_[:], xT_hi[:], xT_lo[:], v_freed, xT_ready)

            def take_q(b):
                bank_ = v_bank()
                if b == 0:
                    dve.wait_ge(rows_loaded, 32)
                else:
                    dve.wait_ge(q_split, 2 * b)
                settle(dve.tensor_scalar(q_full[:], bank_[:], bq, float(D) ** -0.5, ALU.add, ALU.mult))
                dve.sem_inc(v_freed, 1)
                dve.sem_inc(q_ready, 1)

            def take_k(b):
                bank_ = v_bank()
                if b >= 1:
                    dve.wait_ge(k_split, 2 * b)
                settle(dve.tensor_scalar(k_full[:], bank_[:], bk, None, ALU.add))
                dve.sem_inc(v_freed, 1)
                dve.sem_inc(k_ready, 1)

            def take_v(b):
                bank_ = v_bank()
                if b < 2:
                    dve.wait_ge(v_const, 2 * (b + 1))
                else:
                    dve.wait_ge(pv_done, SETS * (b - 1))
                for s in range(SETS):
                    at = 8 * (s % 2)
                    src = bank_[:].rearrange("p (n q s i) -> p n q s i", n=TB, q=QUADS, s=SETS)[:, :, :, s, :]
                    bias = bv_rows.rearrange("p (a q s i) -> p a q s i", a=1, q=QUADS, s=SETS)[:, :, :, s, :]
                    ins = dve.tensor_tensor(v_ones[b % 2][:, :, s, :, at:at + D], src,
                                            bias.to_broadcast([P, TB, QUADS, D]), ALU.add)
                settle(ins)
                dve.sem_inc(v_freed, 1)
                dve.sem_inc(v_ready, 1)

            def max_unit(b, s, k):
                n = SETS * b + s
                q, kind = k // KINDS, k % KINDS
                bank_ = v_bank()
                at = 0
                for t in MAX_BLOCKS[kind]:
                    cols = P * (t + 1)
                    ins = dve.tensor_tensor_reduce(unused[:, (uses[0] - 1) % V_BANKS, at:at + cols],
                                                   bank_[:, at:at + cols],
                                                   cst[:, C_MASK + T - cols:C_MASK + T], 1.0, MASKED,
                                                   ALU.add, ALU.max,
                                                   row_max[:, n % 2, q * TB + t:q * TB + t + 1])
                    at += cols
                ins.then_inc(v_freed, 1)
                if k == UNITS - 1:
                    dve.wait_ge(v_freed, uses[0])
                    dve.sem_inc(max_ready, 1)

            def take_max(b, s):
                n = SETS * b + s
                bank_ = v_bank()
                if n >= 1:
                    dve.wait_ge(m_loaded, 32 * n)
                src = bank_[0:TB * QUADS, 0:P]
                settle(dve.tensor_scalar(m_hi[:], src, -1.0, None, ALU.mult))
                settle(dve.scalar_tensor_tensor(out=m_lo[:], in0=src, scalar=-1.0, in1=m_hi[:].bitcast(F32),
                                                op0=ALU.mult, op1=ALU.subtract))
                dve.sem_inc(v_freed, 1)
                dve.sem_inc(m_ready, 1)

            def take_y(b, half):
                bank_ = v_bank()
                rows = bank_[:].rearrange("p (g r) -> p g r", r=QR)
                settle(dve.reciprocal(rden[:, half, :, :], rows[:, :, 16::8]))
                dst = y_norm[:].rearrange("p (g h e i) -> p g h e i", h=2, e=2, i=D)[:, :, half, :, :]
                settle(dve.tensor_tensor(dst, rows[:, :, 0:16].rearrange("p g (e i) -> p g e i", e=2),
                                         rden[:, half, :, :].unsqueeze(3).to_broadcast([P, TB * QUADS, 2, D]), ALU.mult))
                dve.sem_inc(v_freed, 1)
                dve.sem_inc(y_norm_ready, 1)

            def take_yT(b):
                bank_ = v_bank()
                settle(dve.tensor_copy(yT[:], bank_[:]))
                dve.sem_inc(v_freed, 1)
                dve.sem_inc(yT_ready, 1)

            def take_attention(b):
                bank_ = v_bank()
                dve.wait_ge(xb_ready, b + 1)
                settle(dve.tensor_tensor(x2[b % 2][:], bank_[:].rearrange("p (n c) -> p n c", n=TB), xb_res[:], ALU.add))
                dve.sem_inc(v_freed, 1)
                dve.sem_inc(x2_ready, 1)
                statistics(x2[b % 2], stats2, mv2, z_stats_ready)

            def take_zT(b):
                bank_ = v_bank()
                if b >= 1:
                    dve.wait_ge(g_filled, NT * b)
                split(bank_[:], zT_hi[:], zT_lo[:], v_freed, zT_ready)

            def take_logits(b):
                bank_ = v_bank()
                sums = bank_[:, 0:2 * TB * E].rearrange("p (n a e) -> p n a e", n=TB, a=2)
                settle(dve.tensor_tensor(lg2[:], sums[:, :, 0, :], gate_b_rows.unsqueeze(1).to_broadcast([P, TB, E]),
                                         ALU.add))
                settle(dve.tensor_tensor(lg[:], lg2[:], sums[:, :, 1, :], ALU.add))
                dve.sem_inc(v_freed, 1)
                settle(dve.tensor_tensor(lg2[:], lg[:], lg[:], ALU.mult))
                dve.tensor_reduce(mean_square[:], lg2[:], AX.X, ALU.add).then_inc(square_ready, 1)

            def route(b):
                dve.wait_ge(logits_normed, b + 1)
                settle(dve.tensor_reduce(rt[:, 3, :], lg[:], AX.X, ALU.max))
                dve.tensor_tensor(lg2[:], lg[:], rt[:, 3, :].unsqueeze(2).to_broadcast([P, TB, E]),
                                  ALU.subtract).then_inc(gate_in, 1)

            def take_gates(b):
                dve.wait_ge(gate_exp, b + 1)
                settle(dve.tensor_reduce(rt[:, 0, :], lge[:], AX.X, ALU.add))
                settle(dve.reciprocal(rt[:, 1, :], rt[:, 0, :]))
                settle(dve.tensor_scalar(rt[:, 2, :], rt[:, 1, :], EPS_GATE, None, ALU.add))
                settle(dve.reciprocal(rt[:, 3, :], rt[:, 2, :]))
                settle(dve.tensor_tensor(gate[b % 2][:], rt[:, 1, :], rt[:, 3, :], ALU.mult))

            def take_ffn(b):
                bank_ = v_bank()
                if b >= 1:
                    dve.wait_ge(stored, 16 * b)
                for n in range(TB):
                    ins = dve.scalar_tensor_tensor(out=result[:, n, :], in0=bank_[:, n * P:(n + 1) * P],
                                                   scalar=gate[b % 2][:, n:n + 1], in1=x2[b % 2][:, n, :],
                                                   op0=ALU.mult, op1=ALU.add)
                settle(ins)
                dve.sem_inc(v_freed, 1)
                dve.sem_inc(result_ready, 1)

            def side(b, s, k):
                for stage, of in due(STAGES, b, s, k, B):
                    if stage == "y_low":
                        take_y(of, 0)
                    if stage == "y_high":
                        take_y(of, 1)
                    if stage == "y_norm":
                        take_yT(of)
                    if stage == "attention":
                        take_attention(of)
                    if stage == "z_norm":
                        normalise_z(of)
                    if stage == "z":
                        take_zT(of)
                    if stage == "logits":
                        take_logits(of)
                    if stage == "route":
                        route(of)
                    if stage == "gates":
                        take_gates(of)
                    if stage == "ffn":
                        take_ffn(of)
                    if stage == "b2" and of == 0:
                        dve.tensor_reduce(b2_sum[:], b2_cols, AX.X, ALU.add).then_inc(b2_ready, 1)
                    if stage == "x_stats":
                        take_x(of)
                    if stage == "x_norm":
                        normalise_x(of)
                    if stage == "x":
                        take_xT(of)
                    if stage == "q":
                        take_q(of)
                    if stage == "k":
                        take_k(of)
                    if stage == "v":
                        take_v(of)

            take_x(0)
            root_x()
            normalise_x(0)
            take_xT(0)
            take_q(0)
            take_k(0)
            take_v(0)
            dve.wait_ge(cst_loaded, 16)
            for k in range(UNITS):
                max_unit(0, 0, k)
            take_max(0, 0)
            for k in range(PLACES):
                for unit in maxima_due(-1, k):
                    if unit[1] == 1:
                        max_unit(*unit)
            for b in range(B):
                for s in range(SETS):
                    for k in range(PLACES):
                        side(b, s, k)
                        for unit in maxima_due(SETS * b + s, k):
                            max_unit(*unit)
                        if planned(b, s, k, "take_max") and next_set(b, s)[0] < B:
                            take_max(*next_set(b, s))
            take_y(B - 1, 1)
            take_yT(B - 1)
            take_attention(B - 1)
            root_z(B - 1)
            normalise_z(B - 1)
            take_zT(B - 1)
            take_ffn(B - 2)
            take_logits(B - 1)
            route(B - 1)
            take_gates(B - 1)
            take_ffn(B - 1)


def constants(H, T):
    import numpy as np

    SETS = H // QUADS
    c = np.zeros((P, C_QUAD + QUADS), np.float32)
    c[:, C_IDENT:C_IDENT + P] = np.eye(P)
    c[:, C_MASK + T - P:C_MASK + T] = np.where(np.arange(P)[None, :] > np.arange(P)[:, None], MASKED, 0.0)
    slopes = (2.0 ** (-(8.0 / H) * np.arange(1, H + 1))).astype(np.float32)
    high = (slopes.view(np.uint32) & np.uint32(0xFFFFF000)).view(np.float32)
    c[ALIBI_ROWS:MAX_ROWS, C_KEY:C_KEY + T] = np.arange(T)
    c[MAX_ROWS:MAX_ROWS + 2 * QUADS, C_KEY:C_KEY + T] = 1.0
    for q in range(QUADS):
        heads = slice(QUADS * q, QUADS * q + SETS)
        c[ALIBI_ROWS + q, C_QUERY:C_QUERY + SETS] = high[heads]
        c[ALIBI_ROWS + QUADS + q, C_QUERY:C_QUERY + SETS] = (slopes - high)[heads]
        c[CONST_ROWS + q:P:QUADS, C_QUAD + q] = 1.0
    return c


def qk_order(a):
    import numpy as np

    q, k, v = np.split(a.reshape(-1, 3 * P), 3, 1)
    q = q.reshape(-1, QUADS, 4, 8).swapaxes(-1, -2)
    k = k.reshape(-1, QUADS, 2, 2, 8).swapaxes(-1, -2)
    return np.concatenate([q.reshape(-1, P), k.reshape(-1, P), v], 1).reshape(a.shape)


def kernel(**inputs):
    import numpy as np
    import concourse.bacc as bacc
    from concourse.bass_utils import run_bass_kernel_spmd

    a = {name: np.ascontiguousarray(v) for name, v in inputs.items()}
    x, w1, w2 = a["L0_attn_x"], a["L0_ffn_w1"], a["L0_ffn_w2"]
    E, C, F = w1.shape
    w_attn, b_attn = qk_order(a["L0_attn_w_attn"]), qk_order(a["L0_attn_b_attn"])
    by_tile = lambda v: v.reshape((E * F // P, P) + v.shape[2:]).swapaxes(0, 1)
    arrays = {
        "x": x,
        "w_attn": w_attn,
        "w_proj": a["L0_attn_w_proj"],
        "w1": w1.swapaxes(0, 1).reshape(C, E * F),
        "w2": by_tile(w2),
        "columns": np.concatenate([a["L0_ffn_gate_w"].T, a["L0_ffn_b2"].T, by_tile(a["L0_ffn_b1"]),
                                   b_attn[:2 * C].reshape(2, C).T], 1),
        "rows": np.concatenate([b_attn[2 * C:], a["L0_attn_b_proj"], a["L0_ffn_gate_b"], a["L0_ffn_rms_w"]])[None],
        "consts": constants(16, x.shape[1]),
    }
    arrays = {name: np.ascontiguousarray(v) for name, v in arrays.items()}

    nc = bacc.Bacc("TRN2", target_bir_lowering=False, num_devices=1)
    args = [nc.dram_tensor(name, v.shape, mybir.dt.from_np(v.dtype), kind="ExternalInput").ap()
            for name, v in arrays.items()]
    args.append(nc.dram_tensor("out", x.shape, F32, kind="ExternalOutput").ap())
    block_kernel(nc, *args)
    r = run_bass_kernel_spmd(nc, [arrays], core_ids=[0])
    return r.results[0]["out"]
```
